# Optimizing a Trainium2 kernel written in Bass

```python
import numpy as np
import jax
import jax.numpy as jnp

def _softmax(x, axis=-1):
    return jax.nn.softmax(x, axis=axis)

def _gelu(x):
    return jax.nn.gelu(x, approximate=True)

def _silu(x):
    return jax.nn.silu(x)

def _sigmoid(x):
    return jax.nn.sigmoid(x)

def _layernorm(x, axis=-1, eps=1e-05):
    m = jnp.mean(x, axis=axis, keepdims=True)
    v = jnp.var(x, axis=axis, keepdims=True)
    return (x - m) / jnp.sqrt(v + eps)

def _scatter_add(tgt, idx, src, axis=0):
    return tgt.at[idx].add(src)

def _segment_sum(src, seg, n):
    return jax.ops.segment_sum(src, seg, n)
kernel_name = 'mk_macaron_d1_jaxref_r4_042ac3'

def setup_inputs(seed: int=0):
    np.random.seed(seed)
    _w = jnp.asarray

    def _L0_attn_setup():
        import jax, jax.numpy as jnp
        import numpy as np
        D = 256
        H = 16
        HKV = 4
        HD = D // H
        L = 64
        EPS = 1e-06
        LN_EPS = 1e-05
        B, S = (2, 256)

        def _feat(x):
            return jax.nn.elu(x) + 1.0
        key = jax.random.key(seed)
        ks = jax.random.split(key, 8)
        w = lambda k, shape: jax.random.normal(k, shape, jnp.float32) * 0.02
        return {'x': jax.random.normal(ks[0], (B, S, D), jnp.float32), 'Wq': w(ks[1], (D, D)), 'bq': jnp.zeros((D,), jnp.float32), 'Wk': w(ks[2], (D, HKV * HD)), 'bk': jnp.zeros((HKV * HD,), jnp.float32), 'Wv': w(ks[3], (D, HKV * HD)), 'bv': jnp.zeros((HKV * HD,), jnp.float32), 'Wc': w(ks[4], (HKV * HD, L)), 'We': w(ks[5], (L, HKV * HD)), 'Wo': w(ks[6], (D, D)), 'bo': jnp.zeros((D,), jnp.float32), 'gamma': jnp.ones((D,), jnp.float32), 'beta': jnp.zeros((D,), jnp.float32)}
    _L0_attn_in = _L0_attn_setup()

    def _L0_ffn_setup():
        import jax, jax.numpy as jnp
        import numpy as np
        DIM = 256

        def _reference_tuple_inner(x, W_r, W_k, W_v, mu_r, mu_k):
            B, T, C = x.shape
            x_prev = jnp.concatenate([jnp.zeros((B, 1, C), x.dtype), x[:, :-1, :]], axis=1)
            xr = mu_r * x + (1.0 - mu_r) * x_prev
            xk = mu_k * x + (1.0 - mu_k) * x_prev
            r = jax.nn.sigmoid(jnp.einsum('btc,dc->btd', xr, W_r))
            k = jnp.einsum('btc,dc->btd', xk, W_k)
            k_act = jnp.square(jax.nn.relu(k))
            out = r * jnp.einsum('btc,dc->btd', k_act, W_v)
            new_state = x[:, -1, :]
            return (out, new_state)
        key = jax.random.key(seed)
        ks = jax.random.split(key, 6)
        B, T, C = (8, 512, DIM)
        x = jax.random.normal(ks[0], (B, T, C), dtype=jnp.float32)
        s = 1.0 / np.sqrt(C)
        W_r = jax.random.uniform(ks[1], (C, C), jnp.float32, -s, s)
        W_k = jax.random.uniform(ks[2], (C, C), jnp.float32, -s, s)
        W_v = jax.random.uniform(ks[3], (C, C), jnp.float32, -s, s)
        mu_r = jax.random.uniform(ks[4], (C,), jnp.float32)
        mu_k = jax.random.uniform(ks[5], (C,), jnp.float32)
        return {'x': x, 'W_r': W_r, 'W_k': W_k, 'W_v': W_v, 'mu_r': mu_r, 'mu_k': mu_k}
    _L0_ffn_in = _L0_ffn_setup()
    _d = {'L0_attn_x': _L0_attn_in['x'], 'L0_attn_Wq': _L0_attn_in['Wq'], 'L0_attn_bq': _L0_attn_in['bq'], 'L0_attn_Wk': _L0_attn_in['Wk'], 'L0_attn_bk': _L0_attn_in['bk'], 'L0_attn_Wv': _L0_attn_in['Wv'], 'L0_attn_bv': _L0_attn_in['bv'], 'L0_attn_Wc': _L0_attn_in['Wc'], 'L0_attn_We': _L0_attn_in['We'], 'L0_attn_Wo': _L0_attn_in['Wo'], 'L0_attn_bo': _L0_attn_in['bo'], 'L0_attn_gamma': _L0_attn_in['gamma'], 'L0_attn_beta': _L0_attn_in['beta'], 'L0_ffn_W_r': _L0_ffn_in['W_r'], 'L0_ffn_W_k': _L0_ffn_in['W_k'], 'L0_ffn_W_v': _L0_ffn_in['W_v'], 'L0_ffn_mu_r': _L0_ffn_in['mu_r'], 'L0_ffn_mu_k': _L0_ffn_in['mu_k']}
    _x0 = _d['L0_attn_x']
    _d['L0_attn_x'] = jax.random.normal(jax.random.fold_in(jax.random.key(seed), 1), (8, 1024, 256), dtype=_x0.dtype)
    del _x0
    return _d

def reference(L0_attn_x, L0_attn_Wq, L0_attn_bq, L0_attn_Wk, L0_attn_bk, L0_attn_Wv, L0_attn_bv, L0_attn_Wc, L0_attn_We, L0_attn_Wo, L0_attn_bo, L0_attn_gamma, L0_attn_beta, L0_ffn_W_r, L0_ffn_W_k, L0_ffn_W_v, L0_ffn_mu_r, L0_ffn_mu_k):

    def _L0_attn_ref(x, Wq, bq, Wk, bk, Wv, bv, Wc, We, Wo, bo, gamma, beta):
        import jax, jax.numpy as jnp
        import numpy as np
        D = 256
        H = 16
        HKV = 4
        HD = D // H
        L = 64
        EPS = 1e-06
        LN_EPS = 1e-05
        B, S = (2, 256)

        def _feat(x):
            return jax.nn.elu(x) + 1.0
        b, s, _ = x.shape
        residual = x
        q = x @ Wq + bq
        k = x @ Wk + bk
        v = x @ Wv + bv
        k = k @ Wc @ We
        v = v @ Wc @ We
        q = q.reshape(b, s, H, HD).transpose(0, 2, 1, 3)
        k = k.reshape(b, s, HKV, HD).transpose(0, 2, 1, 3)
        v = v.reshape(b, s, HKV, HD).transpose(0, 2, 1, 3)
        rep = H // HKV
        k = jnp.repeat(k, rep, axis=1)
        v = jnp.repeat(v, rep, axis=1)
        qf = _feat(q)
        kf = _feat(k)
        kv = jnp.einsum('bhsf,bhsd->bhsfd', kf, v)
        kv_cum = jnp.cumsum(kv, axis=2)
        num = jnp.einsum('bhsf,bhsfd->bhsd', qf, kv_cum)
        den = jnp.einsum('bhsf,bhsf->bhs', qf, jnp.cumsum(kf, axis=2))[..., None] + EPS
        o = num / den
        o = o.transpose(0, 2, 1, 3).reshape(b, s, D)
        o = o @ Wo + bo
        y = residual + o
        mu = jnp.mean(y, axis=-1, keepdims=True)
        var = jnp.var(y, axis=-1, keepdims=True)
        return (y - mu) / jnp.sqrt(var + LN_EPS) * gamma + beta

    def _L0_ffn_ref(x, W_r, W_k, W_v, mu_r, mu_k):
        import jax, jax.numpy as jnp
        import numpy as np
        DIM = 256

        def _reference_tuple_inner(x, W_r, W_k, W_v, mu_r, mu_k):
            B, T, C = x.shape
            x_prev = jnp.concatenate([jnp.zeros((B, 1, C), x.dtype), x[:, :-1, :]], axis=1)
            xr = mu_r * x + (1.0 - mu_r) * x_prev
            xk = mu_k * x + (1.0 - mu_k) * x_prev
            r = jax.nn.sigmoid(jnp.einsum('btc,dc->btd', xr, W_r))
            k = jnp.einsum('btc,dc->btd', xk, W_k)
            k_act = jnp.square(jax.nn.relu(k))
            out = r * jnp.einsum('btc,dc->btd', k_act, W_v)
            new_state = x[:, -1, :]
            return (out, new_state)
        return _reference_tuple_inner(x, W_r, W_k, W_v, mu_r, mu_k)[0]
    x = L0_attn_x
    x = x + 0.5 * _L0_ffn_ref(_layernorm(x, axis=-1), L0_ffn_W_r, L0_ffn_W_k, L0_ffn_W_v, L0_ffn_mu_r, L0_ffn_mu_k)
    x = x + _L0_attn_ref(_layernorm(x, axis=-1), L0_attn_Wq, L0_attn_bq, L0_attn_Wk, L0_attn_bk, L0_attn_Wv, L0_attn_bv, L0_attn_Wc, L0_attn_We, L0_attn_Wo, L0_attn_bo, L0_attn_gamma, L0_attn_beta)
    x = x + 0.5 * _L0_ffn_ref(_layernorm(x, axis=-1), L0_ffn_W_r, L0_ffn_W_k, L0_ffn_W_v, L0_ffn_mu_r, L0_ffn_mu_k)
    return x

_drawn_inputs = setup_inputs


def setup_inputs(seed=0):
    import zlib

    import numpy as np

    out = dict(_drawn_inputs(seed))
    spreads = {'L0_attn_bq': (0.0, 2.0),
     'L0_attn_bk': (0.0, 2.0),
     'L0_attn_bv': (0.0, 0.8),
     'L0_attn_bo': (0.0, 0.53),
     'L0_attn_gamma': (1.0, 0.2),
     'L0_attn_beta': (0.0, 0.1)}
    factors = {'L0_attn_Wq': 8.0,
     'L0_attn_Wk': 8.0,
     'L0_attn_Wv': 8.0,
     'L0_attn_Wc': 8.0,
     'L0_attn_We': 8.0,
     'L0_attn_Wo': 8.0,
     'L0_ffn_W_r': 4.256,
     'L0_ffn_mu_r': 8.0}
    for name, (base, spread) in spreads.items():
        noise = np.random.default_rng([zlib.crc32(name.encode()), seed]).standard_normal(out[name].shape)
        drawn = base * np.exp(spread * noise) if base else spread * noise
        out[name] = jnp.asarray(drawn.astype(out[name].dtype))
    for name, factor in factors.items():
        out[name] = (out[name] * factor).astype(out[name].dtype)
    return out
```

```python
from contextlib import ExitStack

import concourse.bass as bass
from concourse import mybir

F32 = mybir.dt.float32
ALU = mybir.AluOpType
ACT = mybir.ActivationFunctionType

P = 128
EPS_LN = 1e-5
EPS_DEN = 1e-6


def macaron_program(nc, x, Wq, bq, Wk, bk, Wv, bv, Wc, We, Wo, bo, gamma, beta, W_r, W_k, W_v, mu_r, mu_k, out):
    B, S, D = x.shape
    KV = Wk.shape[1]
    HD = 16
    J = KV // HD
    G = D // KV
    C = 32
    NC = P // C
    V1 = HD + 1
    VW = J * V1
    CI = D // P
    NB = B // 2
    NT = S // P
    STEPS = NB * NT
    assert D == CI * P and J * C == P and 2 * KV == P and STEPS % 2 == 0

    ctx = ExitStack()
    with ctx:
        def sb(name, *shape):
            return ctx.enter_context(nc.sbuf_tensor(name, list(shape), F32))

        def sem(name):
            return ctx.enter_context(nc.semaphore(name))

        wr_raw, wk_raw, wv_raw = (sb(f"{n}_raw", P, CI, D) for n in ("wr", "wk", "wv"))
        wrT, wkT, wvT = (sb(f"{n}T", P, CI, D) for n in ("wr", "wk", "wv"))
        wq_raw = sb("wq_raw", P, CI, D)
        wqG = sb("wqG", P, CI, G, KV)
        wo_p = sb("wo_p", P, CI, D)
        kraw, vraw = sb("kraw", P, CI, KV), sb("vraw", P, CI, KV)
        krawT, vrawT = sb("krawT", KV, CI, P), sb("vrawT", KV, CI, P)
        wc_sb, we_sb, wcT, wce = (sb(n, KV, KV) for n in ("wc_sb", "we_sb", "wcT", "wce"))
        wkv = sb("wkv", P, CI, 2 * KV)
        bkc, bvc = sb("bkc", KV, 1), sb("bvc", KV, 1)
        bk1_rep, bv_rep = sb("bk1_rep", P, KV), sb("bv_rep", P, KV)
        bq1 = sb("bq1", P, G)
        bo_rep, gamma_rep, beta_rep = sb("bo_rep", P, D), sb("gamma_rep", P, D), sb("beta_rep", P, D)
        mur, muk = sb("mur", P, CI), sb("muk", P, CI)
        ident = sb("ident", P, P)
        causal = sb("causal", P, C)
        vmask = sb("vmask", P, J, V1)
        smask = sb("smask", P, J, V1)
        kmask = sb("kmask", P, J)
        spread = sb("spread", P, NC, J, C)
        eps_ln, spacer = sb("eps_ln", P, 2), sb("spacer", P, 1)
        neg_one = sb("neg_one", P, 2)
        neg_half = sb("neg_half", P, 2)

        class Ffn:
            pass

        def ffn_buffers(n):
            f = Ffn()
            f.stats, f.mv = sb(f"{n}_stats", P, 2, 6), sb(f"{n}_mv", P, 2, 2)
            f.veps, f.rstd = sb(f"{n}_veps", P, 2), sb(f"{n}_rstd", P, 2)
            f.negm, f.nmr = sb(f"{n}_negm", P, 2), sb(f"{n}_nmr", P, 2)
            f.h = sb(f"{n}_h", P, 2, D)
            f.hT = sb(f"{n}_hT", P, CI, 2, P + 1)
            f.carry = sb(f"{n}_carry", P, NT + 1, CI, 2)
            f.d = sb(f"{n}_d", P, CI, 2, P)
            f.xk, f.xr = sb(f"{n}_xk", P, CI, 2, P), sb(f"{n}_xr", P, CI, 2, P)
            f.relu, f.ka = sb(f"{n}_relu", P, CI, 2, P), sb(f"{n}_ka", P, CI, 2, P)
            f.th, f.t1 = sb(f"{n}_th", P, 2, D), sb(f"{n}_t1", P, 2, D)
            f.s = {s: sem(f"{n}_{s}_done") for s in
                   ("stats", "mv", "veps", "rstd", "nmr", "h", "hTp", "hT", "edge", "d", "xk", "xr",
                    "kp", "relu", "ka", "rp", "th", "vp", "t1", "y")}
            return f

        f1, f2 = ffn_buffers("f1"), ffn_buffers("f2")
        x_in = sb("x_in", P, 2, 2, D)
        x1 = sb("x1", P, 2, 2, D)
        x2 = sb("x2", P, 2, 2, D)
        x3 = sb("x3", P, 2, 2, D)
        f1.src, f1.dst, f2.src, f2.dst = x_in, x1, x2, x3

        a_stats, a_mv = sb("a_stats", P, 2, 6), sb("a_mv", P, 2, 2)
        a_veps, a_rstd, a_negm, a_nmr = (sb(f"a_{n}", P, 2) for n in ("veps", "rstd", "negm", "nmr"))
        h2 = sb("h2", P, 2, D)
        h2b = sb("h2b", P, 2, 2, D)
        x1b = sb("x1b", P, 2, 2, D)
        h2T = sb("h2T", P, CI, 2, P)
        yk, ek = sb("yk", P, 2, KV), sb("ek", P, 2, KV)
        kf = sb("kf", P, 2, KV)
        vaug = sb("vaug", P, 2, 2, J, V1)
        kfT = sb("kfT", P, P)
        kbd = sb("kbd", P, NC, J, C)
        yq, eq = sb("yq", P, G, P), sb("eq", P, G, P)
        qf = sb("qf", P, 2, G, P)
        vbd = sb("vbd", P, 2, NC, VW)
        am = sb("am", P, 2, NC, G, C)
        sp = sb("sp", P, NC, VW)
        st = sb("st", P, 2, NC, VW)
        st_carry = sb("st_carry", P, NT + 1, VW)
        den, rden = sb("den", P, 2, J * G), sb("rden", P, 2, J * G)
        attn = sb("attn", P, 2, D)
        attnT = sb("attnT", P, CI, 2, P)
        y = sb("y", P, 2, D)
        y_stats, y_mv = sb("y_stats", P, 2, 6), sb("y_mv", P, 2, 2)
        y_veps, y_rstd = sb("y_veps", P, 2), sb("y_rstd", P, 2)
        z = sb("z", P, 2, D)

        def psum(name):
            return ctx.enter_context(nc.psum_tensor(name, [P, 512], F32))

        bank_T, bank_K, bank_R, bank_V, bank_Q, bank_KV, bank_0, bank_1 = (
            psum(n) for n in ("bank_T", "bank_K", "bank_R", "bank_V", "bank_Q", "bank_KV", "bank_0", "bank_1"))
        psT = bank_T[:, :].rearrange("q (c p t) -> q c p t", c=CI, p=2)
        psK = bank_K[:, :].rearrange("q (c n) -> q c n", c=CI)
        psR = bank_R[:, :].rearrange("q (p d) -> q p d", p=2)
        psV = bank_V[:, :].rearrange("q (p d) -> q p d", p=2)
        psQ = bank_Q[:, :].rearrange("q (g t) -> q g t", g=G)
        psKV = bank_KV[:, 0:4 * KV].rearrange("q (p n) -> q p n", p=2)
        psKT = bank_KV[:, 4 * KV:4 * KV + P]
        psS = bank_KV[:, 0:NC * VW].rearrange("q (c n) -> q c n", c=NC)
        psO = [b[:, 0:G * VW].rearrange("q (g j d) -> q g j d", g=G, j=J) for b in (bank_Q, bank_KV)]
        psVB = [b[:, 0:NC * VW].rearrange("q (c n) -> q c n", c=NC) for b in (bank_0, bank_1)]
        psA = [b[:, :].rearrange("q (c g t) -> q c g t", c=NC, g=G) for b in (bank_0, bank_1)]
        psW = bank_0[:, :].rearrange("q (p d) -> q p d", p=2)

        w_loaded = sem("w_loaded")
        x_loaded, stored = [sem("x_loaded0"), sem("x_loaded1")], [sem("stored0"), sem("stored1")]
        consts = sem("consts")
        mask_step = sem("mask_step")
        setup_pe, setup_dve = sem("setup_pe"), sem("setup_dve")
        A = {n: sem(f"a_{n}_done") for n in (
            "stats", "mv", "veps", "rstd", "nmr", "h", "hTp", "hT", "h2b", "x1b", "kvp", "qp", "yk", "vaug",
            "ek", "kf", "kTp", "kT", "kbd", "yq", "eq", "qf", "vb0p", "vb1p", "vb0", "vb1", "Sp", "sp",
            "st0", "st", "stc", "A0p", "A1p", "A0", "A1", "O0p", "O1p", "den0", "den1", "rden0", "rden1",
            "o0", "o1", "oTp", "oT", "wp", "y", "ystats", "ymv", "yveps", "yrstd", "z", "x2")}

        x_dram = x.rearrange("(p b) (n t) c -> b n t p c", p=2, t=P)
        out_dram = out.rearrange("(p b) (n t) c -> b n t p c", p=2, t=P)
        loads = []

        def row(v):
            return v.rearrange("(a c) -> a c", a=1)

        for dst, src in ((wr_raw, W_r), (wk_raw, W_k), (wv_raw, W_v), (wq_raw, Wq), (kraw, Wk), (vraw, Wv)):
            loads.append((dst[:], src.rearrange("(o q) c -> q o c", q=P)))
        for dst, src in ((wc_sb, Wc), (we_sb, We)):
            loads.append((dst[:], src))
        for g in range(G):
            for j in range(J):
                q0 = (g % 2) * KV + j * HD
                loads.append((wo_p[q0:q0 + HD, g // 2, :], Wo[(j * G + g) * HD:(j * G + g + 1) * HD, :]))
        for dst, src in ((bkc, bk), (bvc, bv)):
            loads.append((dst[:], src.rearrange("(q a) -> q a", a=1)))
        for p in range(2):
            for j in range(J):
                q0 = p * KV + j * HD
                loads.append((bq1[q0:q0 + HD, :],
                              bq.rearrange("(j g f) -> j f g", j=J, g=G)[j]))
        for dst, src in ((bo_rep, bo), (gamma_rep, gamma), (beta_rep, beta)):
            loads.append((dst[:], row(src).broadcast_to([P, D])))
        for dst, src in ((mur, mu_r), (muk, mu_k)):
            loads.append((dst[:], src.rearrange("(c q) -> q c", q=P)))
        W_ALL = 16 * len(loads)

        LAST = STEPS - 1

        def iterations(eng, body):
            for i in (-1, 0, 1, 2, 3):
                body(i, i % 2)
            with eng.Fori(2, STEPS // 2 - 1) as m:
                for u in range(2):
                    body(m * 2 + u, u)
            for i in range(STEPS - 2, STEPS + 3):
                body(i, i % 2)

        def has(k):
            return not isinstance(k, int) or 0 <= k <= LAST

        def upto(k):
            return min(k, LAST) + 1 if isinstance(k, int) else k + 1

        block = ctx.enter_context(nc.Block())

        @block.sync
        def _(sp_eng):
            def load(k, u):
                sp_eng.dma_start(x_in[:, u], x_dram[k // NT, k % NT]).then_inc(x_loaded[u], 16)

            load(0, 0)
            for dst, src in loads:
                sp_eng.dma_start(dst, src, allow_slow_non_contiguous=True).then_inc(w_loaded, 16)
            load(1, 1)

            def body(i, u):
                if has(i) and has(i + 2):
                    sp_eng.wait_ge(f1.s["y"], upto(i))
                    load(i + 2, u)

            for i in (0, 1):
                body(i, i % 2)
            with sp_eng.Fori(1, STEPS // 2 - 1) as m:
                for u in range(2):
                    body(m * 2 + u, u)

        @block.tensor
        def _(pe):
            mm, tr = nc.tensor.matmul, nc.tensor.transpose

            pe.wait_ge(consts, 1)
            pe.wait_ge(w_loaded, W_ALL)
            for raw, bank in ((wr_raw, bank_T), (wk_raw, bank_K), (wv_raw, bank_R)):
                for ci in range(CI):
                    for do in range(CI):
                        last = tr(bank[:, ci * D + do * P:ci * D + (do + 1) * P],
                                  raw[:, do, ci * P:(ci + 1) * P], ident[:])
                last.then_inc(setup_pe, 1)
            for raw, bank in ((kraw, bank_V), (vraw, bank_Q)):
                for ci in range(CI):
                    last = tr(bank[0:KV, ci * P:(ci + 1) * P], raw[:, ci, :], ident[:])
                last.then_inc(setup_pe, 1)
            tr(bank_KV[0:KV, 0:KV], wc_sb[:], ident[0:KV, 0:KV]).then_inc(setup_pe, 1)
            pe.wait_ge(setup_dve, 6)
            mm(bank_0[0:KV, 0:KV], wcT[:], we_sb[:], start=True, stop=True).then_inc(setup_pe, 1)
            pe.wait_ge(setup_dve, 7)
            for ci in range(CI):
                for n, t in enumerate((krawT, vrawT)):
                    o = ci * 2 * KV + n * KV
                    last = mm(bank_1[:, o:o + KV], t[:, ci, :], wce[:], start=True, stop=True)
            last.then_inc(setup_pe, 1)
            for n, b in enumerate((bkc, bvc)):
                last = mm(bank_KV[:, n * KV:(n + 1) * KV], b[:].broadcast_to([KV, P]), wce[:],
                          start=True, stop=True)
            last.then_inc(setup_pe, 1)
            pe.wait_ge(setup_dve, 14)

            def ffn_T(f, k, prev_T, prev_count):
                pe.wait_ge(f.s["h"], upto(k))
                if prev_T is not None:
                    pe.wait_ge(prev_T, prev_count)
                for p in range(2):
                    for ci in range(CI):
                        last = tr(psT[:, ci, p, :], f.h[:, p, ci * P:(ci + 1) * P], ident[:])
                last.then_inc(f.s["hTp"], 1)

            def ffn_K(f, k, bank_user, bank_count):
                pe.wait_ge(f.s["xk"], upto(k))
                if bank_user is not None:
                    pe.wait_ge(bank_user, bank_count)
                for co in range(CI):
                    for ci in range(CI):
                        last = mm(psK[:, co, :], wkT[:, ci, co * P:(co + 1) * P],
                                  f.xk[:, ci].rearrange("q p t -> q (p t)"), start=ci == 0, stop=ci == CI - 1)
                last.then_inc(f.s["kp"], 1)

            def ffn_R(f, k, bank_user, bank_count):
                pe.wait_ge(f.s["xr"], upto(k))
                if bank_user is not None:
                    pe.wait_ge(bank_user, bank_count)
                for p in range(2):
                    for ci in range(CI):
                        last = mm(psR[:, p, :], f.xr[:, ci, p, :], wrT[:, ci, :], start=ci == 0, stop=ci == CI - 1)
                last.then_inc(f.s["rp"], 1)

            def ffn_V(f, k, bank_user, bank_count):
                pe.wait_ge(f.s["ka"], upto(k))
                if bank_user is not None:
                    pe.wait_ge(bank_user, bank_count)
                for p in range(2):
                    for ci in range(CI):
                        last = mm(psV[:, p, :], f.ka[:, ci, p, :], wvT[:, ci, :], start=ci == 0, stop=ci == CI - 1)
                last.then_inc(f.s["vp"], 1)

            def body(i, u):
                a, b, c = i, i - 1, i - 2
                if has(b):
                    pe.wait_ge(A["h"], upto(b))
                    pe.wait_ge(f1.s["hT"], upto(b + 1))
                    for p in range(2):
                        for ci in range(CI):
                            last = tr(psT[:, ci, p, :], h2[:, p, ci * P:(ci + 1) * P], ident[:])
                    last.then_inc(A["hTp"], 1)
                if has(a):
                    ffn_K(f1, a, *((f2.s["relu"], upto(a - 3)) if has(a - 3) else (None, 0)))
                if has(b):
                    pe.wait_ge(A["hT"], upto(b))
                    if has(b - 1):
                        pe.wait_ge(A["o1"], upto(b - 1))
                    for p in range(2):
                        for ci in range(CI):
                            last = mm(psKV[:, p, :], h2T[:, ci, p, :], wkv[:, ci, :], start=ci == 0, stop=ci == CI - 1)
                    last.then_inc(A["kvp"], 1)
                    if has(b - 1):
                        pe.wait_ge(A["o0"], upto(b - 1))
                    for g in range(G):
                        for ci in range(CI):
                            for p in range(2):
                                last = mm(psQ[p * KV:(p + 1) * KV, g, :], wqG[:, ci, g, :], h2T[:, ci, p, :],
                                          start=ci == 0, stop=ci == CI - 1)
                    last.then_inc(A["qp"], 1)
                if has(a):
                    ffn_R(f1, a, *((f2.s["th"], upto(a - 3)) if has(a - 3) else (None, 0)))
                if has(b):
                    pe.wait_ge(A["kf"], upto(b))
                    tr(psKT, kf[:].rearrange("q p n -> q (p n)"), ident[:]).then_inc(A["kTp"], 1)
                    for p, bank_free in ((0, "y"), (1, "A1")):
                        pe.wait_ge(A["vaug"], upto(b))
                        if has(b - 1):
                            pe.wait_ge(A[bank_free], upto(b - 1))
                        for n in range(NC):
                            last = mm(psVB[p][:, n, :],
                                      spread[:, n].rearrange("q j s -> q (j s)"),
                                      vaug[:, 1 - u, p].rearrange("q j d -> q (j d)"), start=True, stop=True)
                        last.then_inc(A[f"vb{p}p"], 1)
                if has(c):
                    ffn_T(f2, c, A["hT"], upto(c + 1))
                if has(b):
                    pe.wait_ge(A["kT"], upto(b))
                    for n in range(NC):
                        for p in range(2):
                            last = mm(psS[p * KV:(p + 1) * KV, n, :], kf[0:(n + 1) * C, p, :],
                                      vaug[0:(n + 1) * C, 1 - u, p].rearrange("q j d -> q (j d)"),
                                      start=True, stop=True)
                    last.then_inc(A["Sp"], 1)
                if has(a):
                    ffn_V(f1, a, *((f2.s["t1"], upto(a - 3)) if has(a - 3) else (None, 0)))
                if has(b):
                    for p in range(2):
                        pe.wait_ge(A["qf"], upto(b))
                        pe.wait_ge(A["kbd"], upto(b))
                        pe.wait_ge(A[f"vb{p}"], upto(b))
                        for n in range(NC):
                            last = mm(psA[p][:, n].rearrange("q g t -> q (g t)"),
                                      kbd[p * KV:(p + 1) * KV, n].rearrange("q j s -> q (j s)"),
                                      qf[p * KV:(p + 1) * KV, 1 - u, :, n * C:(n + 1) * C], start=True, stop=True)
                        last.then_inc(A[f"A{p}p"], 1)
                if has(c):
                    ffn_K(f2, c, f1.s["relu"], upto(c + 2))

                def attend(p):
                    pe.wait_ge(A[f"A{p}"], upto(b))
                    pe.wait_ge(A["st"], upto(b))
                    for g in range(G):
                        for n in range(NC):
                            mm(psO[p][n * C:(n + 1) * C, g].rearrange("q j d -> q (j d)"), am[:, p, n, g, :],
                               vbd[:, p, n, :], start=g == 0, stop=False, skip_group_check=True,
                               tile_position=(0, n * C))
                    for g in range(G):
                        for n in range(NC):
                            last = mm(psO[p][n * C:(n + 1) * C, g].rearrange("q j d -> q (j d)"),
                                      qf[p * KV:(p + 1) * KV, 1 - u, g, n * C:(n + 1) * C],
                                      st[p * KV:(p + 1) * KV, 1 - u, n, :], start=False, stop=g == G - 1,
                                      skip_group_check=True, tile_position=(p * KV, n * C))
                    last.then_inc(A[f"O{p}p"], 1)

                if has(b):
                    attend(0)
                if has(c):
                    ffn_R(f2, c, f1.s["th"], upto(c + 2))
                if has(b):
                    attend(1)
                if has(a + 1):
                    ffn_T(f1, a + 1, *((A["oT"], upto(a - 2)) if has(a - 2) else (None, 0)))
                if has(c):
                    ffn_V(f2, c, f1.s["t1"], upto(c + 2))
                if has(b):
                    pe.wait_ge(A["o0"], upto(b))
                    pe.wait_ge(A["o1"], upto(b))
                    pe.wait_ge(f1.s["hT"], upto(b + 2))
                    for p in range(2):
                        for ci in range(CI):
                            last = tr(psT[:, ci, p, :], attn[:, p, ci * P:(ci + 1) * P], ident[:])
                    last.then_inc(A["oTp"], 1)
                    pe.wait_ge(A["oT"], upto(b))
                    for p in range(2):
                        for ci in range(CI):
                            last = mm(psW[:, p, :], attnT[:, ci, p, :], wo_p[:, ci, :], start=ci == 0, stop=ci == CI - 1)
                    last.then_inc(A["wp"], 1)

            iterations(pe, body)

        @block.scalar
        def _(act):
            activation = nc.scalar.activation

            def normalise(s, k, dst, src, rstd, nmr):
                act.wait_ge(s["nmr"], upto(k))
                for p in range(2):
                    last = activation(dst[:, p, :], src[:, p, :], ACT.Identity, bias=nmr[:, p:p + 1],
                                      scale=rstd[:, p:p + 1])
                last.then_inc(s["h"], 1)

            def evacuate_hT(f, k):
                act.wait_ge(f.s["hTp"], upto(k))
                activation(f.hT[:, :, :, 1:], psT, ACT.Copy).then_inc(f.s["hT"], 1)

            def k_activation(f, k):
                act.wait_ge(f.s["kp"], upto(k))
                activation(f.relu[:].rearrange("q c p t -> q (c p t)"), bank_K[:, :], ACT.Relu).then_inc(f.s["relu"], 1)
                act.wait_ge(f.s["relu"], upto(k))
                activation(f.ka[:], f.relu[:], ACT.Square).then_inc(f.s["ka"], 1)

            def r_activation(f, k):
                act.wait_ge(f.s["rp"], upto(k))
                activation(f.th[:], psR, ACT.Tanh, scale=0.5).then_inc(f.s["th"], 1)

            def body(i, u):
                a, b, c = i, i - 1, i - 2
                if has(b):
                    act.wait_ge(A["hTp"], upto(b))
                    activation(h2T[:], psT, ACT.Copy).then_inc(A["hT"], 1)
                if has(a):
                    k_activation(f1, a)
                if has(b):
                    act.wait_ge(A["yk"], upto(b))
                    activation(ek[:], yk[:], ACT.Exp, bias=-1.0).then_inc(A["ek"], 1)
                if has(c):
                    normalise(f2.s, c, f2.h, x2[:, u], f2.rstd, f2.nmr)
                if has(b):
                    act.wait_ge(A["yq"], upto(b))
                    activation(eq[:], yq[:], ACT.Exp, bias=-1.0).then_inc(A["eq"], 1)
                if has(a):
                    r_activation(f1, a)
                if has(b):
                    act.wait_ge(A["kTp"], upto(b))
                    activation(kfT[:], psKT, ACT.Copy).then_inc(A["kT"], 1)
                if has(c):
                    evacuate_hT(f2, c)
                if has(a + 1):
                    normalise(f1.s, a + 1, f1.h, x_in[:, 1 - u], f1.rstd, f1.nmr)
                if has(c):
                    k_activation(f2, c)
                    r_activation(f2, c)
                if has(a):
                    normalise(A, a, h2, x1[:, u], a_rstd, a_nmr)
                if has(a + 1):
                    evacuate_hT(f1, a + 1)
                if has(b):
                    act.wait_ge(A["oTp"], upto(b))
                    activation(attnT[:], psT, ACT.Copy).then_inc(A["oT"], 1)
                if has(c):
                    act.wait_ge(f2.s["y"], upto(c))
                    act.dma_start(out_dram[c // NT, c % NT], x3[:, u]).then_inc(stored[u], 16)

            iterations(act, body)
            for u in range(2):
                act.wait_ge(stored[u], 16 * (STEPS // 2))

        @block.vector
        def _(dve):
            v = nc.vector

            dve.wait_ge(setup_pe, 1)
            v.tensor_copy(wrT[:].rearrange("q c d -> q (c d)"), bank_T[:, :]).then_inc(setup_dve, 1)
            dve.wait_ge(setup_pe, 2)
            v.tensor_copy(wkT[:].rearrange("q c d -> q (c d)"), bank_K[:, :]).then_inc(setup_dve, 1)
            dve.wait_ge(setup_pe, 3)
            v.tensor_scalar(wvT[:].rearrange("q c d -> q (c d)"), bank_R[:, :], 0.25, None, ALU.mult).then_inc(setup_dve, 1)
            for n, (t, bank) in enumerate(((krawT, bank_V), (vrawT, bank_Q))):
                dve.wait_ge(setup_pe, 4 + n)
                v.tensor_copy(t[:].rearrange("q c d -> q (c d)"), bank[0:KV, 0:CI * P]).then_inc(setup_dve, 1)
            dve.wait_ge(setup_pe, 6)
            v.tensor_copy(wcT[:], bank_KV[0:KV, 0:KV]).then_inc(setup_dve, 1)
            dve.wait_ge(setup_pe, 7)
            v.tensor_copy(wce[:], bank_0[0:KV, 0:KV]).then_inc(setup_dve, 1)
            dve.wait_ge(setup_pe, 8)
            v.tensor_copy(wkv[:].rearrange("q c d -> q (c d)"), bank_1[:, 0:CI * 2 * KV]).then_inc(setup_dve, 1)
            dve.wait_ge(setup_pe, 9)
            v.tensor_scalar(bk1_rep[:], bank_KV[:, 0:KV], 1.0, None, ALU.add).then_inc(setup_dve, 1)
            v.tensor_copy(bv_rep[:], bank_KV[:, KV:2 * KV]).then_inc(setup_dve, 1)
            for ci in range(CI):
                v.tensor_copy(wqG[:, ci], wq_raw[:, ci].rearrange("q (j g f) -> q g j f", j=J, g=G)).then_inc(setup_dve, 1)
            v.tensor_scalar(bq1[:], bq1[:], 1.0, None, ALU.add).then_inc(setup_dve, 1)
            dve.wait_ge(consts, 2)
            v.tensor_copy(spread[:], ident[:].rearrange("q (c s) -> q c s", c=NC).unsqueeze(2)
                          .broadcast_to([P, NC, J, C])).then_inc(setup_dve, 1)
            dve.wait_ge(setup_dve, 14)

            def statistics(src, stats, mv, s, stats_name, mv_name, k):
                for p in range(2):
                    last = v.bn_stats(stats[:, p, :], src[:, p, :])
                last.then_inc(s[stats_name], 1)
                dve.wait_ge(s[stats_name], upto(k))
                v.memset(spacer[:], 0.0)
                for p in range(2):
                    last = v.bn_aggr(mv[:, p, :], stats[:, p, :])
                last.then_inc(s[mv_name], 1)

            def mix(f, k, dst, mu, name):
                for ci in range(CI):
                    last = v.scalar_tensor_tensor(out=dst[:, ci], in0=f.d[:, ci], scalar=mu[:, ci:ci + 1],
                                                  in1=f.hT[:, ci, :, 0:P], op0=ALU.mult, op1=ALU.add)
                last.then_inc(f.s[name], 1)

            def mixes(f, k):
                dve.wait_ge(f.s["d"], upto(k))
                mix(f, k, f.xk, muk, "xk")
                mix(f, k, f.xr, mur, "xr")

            def gate(f, k):
                dve.wait_ge(f.s["th"], upto(k))
                dve.wait_ge(f.s["vp"], upto(k))
                v.scalar_tensor_tensor(out=f.t1[:], in0=f.th[:], scalar=1.0, in1=psV, op0=ALU.add,
                                       op1=ALU.mult).then_inc(f.s["t1"], 1)

            def normalise_attention(p, b):
                dve.wait_ge(A[f"O{p}p"], upto(b))
                v.tensor_scalar(den[:, p].rearrange("q (g j) -> q g j", g=G), psO[p][:, :, :, HD], EPS_DEN, None,
                                ALU.add).then_inc(A[f"den{p}"], 1)
                dve.wait_ge(A[f"den{p}"], upto(b))
                v.reciprocal(rden[:, p], den[:, p]).then_inc(A[f"rden{p}"], 1)
                dve.wait_ge(A[f"rden{p}"], upto(b))
                v.tensor_tensor(attn[:, p].rearrange("q (n d) -> q n d", d=HD),
                                psO[p].rearrange("q g j d -> q (g j) d")[:, :, 0:HD],
                                rden[:, p].unsqueeze(2).broadcast_to([P, J * G, HD]),
                                ALU.mult).then_inc(A[f"o{p}"], 1)

            def body(i, u):
                a, b, c = i, i - 1, i - 2
                if has(a):
                    mixes(f1, a)
                if has(c):
                    dve.wait_ge(A["h2b"], upto(c))
                    dve.wait_ge(A["wp"], upto(c))
                    v.tensor_tensor(y[:], psW, h2b[:, u], ALU.add).then_inc(A["y"], 1)
                    dve.wait_ge(A["y"], upto(c))
                    statistics(y, y_stats, y_mv, A, "ystats", "ymv", c)
                if has(b):
                    dve.wait_ge(A["kvp"], upto(b))
                    v.tensor_tensor(yk[:], psKV[:, :, 0:KV], bk1_rep[:].unsqueeze(1).broadcast_to([P, 2, KV]),
                                    ALU.add).then_inc(A["yk"], 1)
                    for p in range(2):
                        last = v.tensor_tensor(vaug[:, 1 - u, p, :, 0:HD],
                                               psKV[:, p, KV:2 * KV].rearrange("q (j d) -> q j d", j=J),
                                               bv_rep[:].rearrange("q (j d) -> q j d", j=J), ALU.add)
                    last.then_inc(A["vaug"], 1)
                if has(c):
                    dve.wait_ge(A["yrstd"], upto(c))
                    for p in range(2):
                        last = v.scalar_tensor_tensor(out=z[:, p], in0=y[:, p], scalar=y_mv[:, p, 0:1],
                                                      in1=gamma_rep[:], op0=ALU.subtract, op1=ALU.mult)
                    last.then_inc(A["z"], 1)
                    dve.wait_ge(A["x1b"], upto(c))
                    dve.wait_ge(A["z"], upto(c))
                    for p in range(2):
                        last = v.scalar_tensor_tensor(out=x2[:, u, p], in0=z[:, p], scalar=y_rstd[:, p:p + 1],
                                                      in1=x1b[:, u, p], op0=ALU.mult, op1=ALU.add)
                    last.then_inc(A["x2"], 1)
                if has(b):
                    dve.wait_ge(A["ek"], upto(b))
                    v.scalar_tensor_tensor(out=kf[:], in0=yk[:], scalar=1.0, in1=ek[:], op0=ALU.max,
                                           op1=ALU.min).then_inc(A["kf"], 1)
                if has(c):
                    dve.wait_ge(A["x2"], upto(c))
                    statistics(x2[:, u], f2.stats, f2.mv, f2.s, "stats", "mv", c)
                if has(b):
                    dve.wait_ge(A["qp"], upto(b))
                    v.tensor_tensor(yq[:], psQ, bq1[:].unsqueeze(2).broadcast_to([P, G, P]),
                                    ALU.add).then_inc(A["yq"], 1)
                    dve.wait_ge(A["eq"], upto(b))
                    v.scalar_tensor_tensor(out=qf[:, 1 - u], in0=yq[:], scalar=1.0, in1=eq[:], op0=ALU.max,
                                           op1=ALU.min).then_inc(A["qf"], 1)
                    for p in range(2):
                        dve.wait_ge(A[f"vb{p}p"], upto(b))
                        v.tensor_tensor(vbd[:, p], psVB[p],
                                        vmask[:].rearrange("q j d -> q (j d)").unsqueeze(1).broadcast_to([P, NC, VW]),
                                        ALU.mult).then_inc(A[f"vb{p}"], 1)
                    dve.wait_ge(A["Sp"], upto(b))
                    v.tensor_tensor(sp[:], psS,
                                    smask[:].rearrange("q j d -> q (j d)").unsqueeze(1).broadcast_to([P, NC, VW]),
                                    ALU.mult).then_inc(A["sp"], 1)
                if has(c):
                    mixes(f2, c)
                if has(a):
                    gate(f1, a)
                if has(b):
                    for p in range(2):
                        dve.wait_ge(A[f"A{p}p"], upto(b))
                        v.tensor_tensor(am[:, p].rearrange("q c g t -> q (c g) t"),
                                        psA[p].rearrange("q c g t -> q (c g) t"),
                                        causal[:].unsqueeze(1).broadcast_to([P, NC * G, C]),
                                        ALU.mult).then_inc(A[f"A{p}"], 1)
                if has(a + 1):
                    dve.wait_ge(x_loaded[1 - u], 16 * ((a + 1) // 2 + 1))
                    statistics(x_in[:, 1 - u], f1.stats, f1.mv, f1.s, "stats", "mv", a + 1)
                if has(a):
                    dve.wait_ge(f1.s["y"], upto(a))
                    statistics(x1[:, u], a_stats, a_mv, A, "stats", "mv", a)
                if has(b):
                    normalise_attention(0, b)
                    normalise_attention(1, b)
                if has(c):
                    gate(f2, c)

            iterations(dve, body)

        @block.gpsimd
        def _(pool):
            g_ = nc.gpsimd

            count = [0]

            def in_turn(ins):
                count[0] += 1
                ins.then_inc(mask_step, 1)
                pool.wait_ge(mask_step, count[0])

            def keep(t, base, pattern, channel):
                in_turn(g_.affine_select(out=t, in_=t, compare_op=ALU.is_ge, fill=0.0, base=base, pattern=pattern,
                                         channel_multiplier=channel))

            in_turn(g_.memset(ident[:], 0.0))
            g_.affine_select(out=ident[:], in_=ident[:], compare_op=ALU.not_equal, fill=1.0, base=0,
                             pattern=[[-1, P]], channel_multiplier=1).then_inc(consts, 1)
            for t in (causal, vmask, smask, kmask):
                in_turn(g_.memset(t[:], 1.0))
            for j in range(J):
                keep(causal[j * C:(j + 1) * C], 0, [[1, C]], -1)
            keep(vmask[:], 0, [[-C, J], [0, V1]], 1)
            keep(vmask[:], C - 1, [[C, J], [0, V1]], -1)
            for p in range(2):
                q = slice(p * KV, (p + 1) * KV)
                keep(smask[q], 0, [[-HD, J], [0, V1]], 1)
                keep(smask[q], HD - 1, [[HD, J], [0, V1]], -1)
                keep(kmask[q], 0, [[-HD, J]], 1)
                keep(kmask[q], HD - 1, [[HD, J]], -1)
            for f in (f1, f2):
                in_turn(g_.memset(f.carry[:, 0], 0.0))
            in_turn(g_.memset(st_carry[:, 0], 0.0))
            in_turn(g_.memset(eps_ln[:], EPS_LN))
            in_turn(g_.memset(neg_one[:], -1.0))
            in_turn(g_.memset(neg_half[:], -0.5))
            g_.memset(vaug[:, :, :, :, HD:], 1.0).then_inc(consts, 1)
            pool.wait_ge(consts, 2)
            pool.wait_ge(w_loaded, W_ALL)

            def inverse_deviation(s, names, mv, veps, rstd, k):
                g_.tensor_tensor(veps[:], mv[:, :, 1], eps_ln[:], ALU.add).then_inc(s[names[0]], 1)
                pool.wait_ge(s[names[0]], upto(k))
                g_.tensor_tensor(rstd[:], veps[:], neg_half[:], ALU.pow).then_inc(s[names[1]], 1)

            def norm_factors(s, mv, veps, rstd, negm, nmr, k):
                pool.wait_ge(s["mv"], upto(k))
                g_.tensor_tensor(negm[:], mv[:, :, 0], neg_one[:], ALU.mult)
                inverse_deviation(s, ("veps", "rstd"), mv, veps, rstd, k)
                pool.wait_ge(s["rstd"], upto(k))
                g_.tensor_tensor(nmr[:], negm[:], rstd[:], ALU.mult).then_inc(s["nmr"], 1)

            def difference(f, k):
                n = k % NT
                pool.wait_ge(f.s["hT"], upto(k))
                g_.tensor_copy(f.hT[:, :, :, 0], f.carry[:, n]).then_inc(f.s["edge"], 1)
                g_.tensor_copy(f.carry[:, n + 1], f.hT[:, :, :, P])
                pool.wait_ge(f.s["edge"], upto(k))
                g_.tensor_tensor(f.d[:], f.hT[:, :, :, 1:], f.hT[:, :, :, 0:P], ALU.subtract).then_inc(f.s["d"], 1)

            def residual(f, k, u):
                pool.wait_ge(f.s["t1"], upto(k))
                g_.tensor_tensor(f.dst[:, u], f.src[:, u], f.t1[:], ALU.add).then_inc(f.s["y"], 1)

            def body(i, u):
                a, b, c = i, i - 1, i - 2
                if has(c):
                    pool.wait_ge(A["ymv"], upto(c))
                    inverse_deviation(A, ("yveps", "yrstd"), y_mv, y_veps, y_rstd, c)
                    norm_factors(f2.s, f2.mv, f2.veps, f2.rstd, f2.negm, f2.nmr, c)
                if has(b):
                    pool.wait_ge(A["kT"], upto(b))
                    g_.tensor_tensor(kbd[:], kfT[:].rearrange("q (c s) -> q c s", c=NC).unsqueeze(2).broadcast_to([P, NC, J, C]),
                                     kmask[:].unsqueeze(1).unsqueeze(3).broadcast_to([P, NC, J, C]),
                                     ALU.mult).then_inc(A["kbd"], 1)
                    n = b % NT
                    g_.tensor_copy(st[:, 1 - u, 0], st_carry[:, n]).then_inc(A["st0"], 1)
                    pool.wait_ge(A["sp"], upto(b))
                    pool.wait_ge(A["st0"], upto(b))
                    g_.tensor_tensor(st[:, 1 - u, 1:], sp[:, 0:NC - 1],
                                     st[:, 1 - u, 0].unsqueeze(1).broadcast_to([P, NC - 1, VW]),
                                     ALU.add).then_inc(A["st"], 1)
                    g_.tensor_tensor(st_carry[:, n + 1], sp[:, NC - 1], st[:, 1 - u, 0], ALU.add).then_inc(A["stc"], 1)
                if has(c):
                    difference(f2, c)
                if has(a):
                    residual(f1, a, u)
                if has(a + 1):
                    norm_factors(f1.s, f1.mv, f1.veps, f1.rstd, f1.negm, f1.nmr, a + 1)
                if has(a):
                    norm_factors(A, a_mv, a_veps, a_rstd, a_negm, a_nmr, a)
                    pool.wait_ge(A["h"], upto(a))
                    g_.tensor_tensor(h2b[:, u], h2[:], bo_rep[:].unsqueeze(1).broadcast_to([P, 2, D]),
                                     ALU.add).then_inc(A["h2b"], 1)
                    g_.tensor_tensor(x1b[:, u], x1[:, u], beta_rep[:].unsqueeze(1).broadcast_to([P, 2, D]),
                                     ALU.add).then_inc(A["x1b"], 1)
                if has(a + 1):
                    difference(f1, a + 1)
                if has(c):
                    if has(c - 2):
                        pool.wait_ge(stored[u], 16 * (c // 2))
                    residual(f2, c, u)

            iterations(pool, body)


_INS = ['L0_attn_x', 'L0_attn_Wq', 'L0_attn_bq', 'L0_attn_Wk', 'L0_attn_bk', 'L0_attn_Wv', 'L0_attn_bv',
        'L0_attn_Wc', 'L0_attn_We', 'L0_attn_Wo', 'L0_attn_bo', 'L0_attn_gamma', 'L0_attn_beta',
        'L0_ffn_W_r', 'L0_ffn_W_k', 'L0_ffn_W_v', 'L0_ffn_mu_r', 'L0_ffn_mu_k']


def kernel(**inputs):
    import numpy as _np
    import concourse.bacc as _bacc
    from concourse import mybir as _mybir
    from concourse.bass_utils import run_bass_kernel_spmd as _run

    nc = _bacc.Bacc("TRN2", target_bir_lowering=False, num_devices=1)
    arrays, args = {}, []
    for name in _INS:
        a = _np.ascontiguousarray(inputs[name])
        arrays[f"in_{name}_dram"] = a
        args.append(nc.dram_tensor(f"in_{name}_dram", a.shape, _mybir.dt.from_np(a.dtype), kind="ExternalInput").ap())
    shape = inputs['L0_attn_x'].shape
    args.append(nc.dram_tensor("out_0_dram", shape, _mybir.dt.float32, kind="ExternalOutput").ap())
    macaron_program(nc, *args)
    r = _run(nc, [arrays], core_ids=[0])
    return r.results[0]["out_0_dram"]
```

```python
from contextlib import ExitStack

import concourse.bass as bass
from concourse import mybir

F32 = mybir.dt.float32
F32R = mybir.dt.float32r
ALU = mybir.AluOpType
ACT = mybir.ActivationFunctionType

P = 128
EPS_LN = 1e-5
EPS_DEN = 1e-6


def macaron_program(nc, x, Wq, bq, Wk, bk, Wv, bv, Wc, We, Wo, bo, gamma, beta, W_r, W_k, W_v, mu_r, mu_k, out):
    B, S, D = x.shape
    KV = Wk.shape[1]
    HD = 16
    J = KV // HD
    G = D // KV
    C = 32
    NC = P // C
    V1 = HD + 1
    VW = J * V1
    CI = D // P
    NB = B // 2
    NT = S // P
    STEPS = NB * NT
    assert D == CI * P and J * C == P and 2 * KV == P and STEPS % 2 == 0

    ctx = ExitStack()
    with ctx:
        def sb(name, *shape):
            return ctx.enter_context(nc.sbuf_tensor(name, list(shape), F32))

        def sbr(name, *shape):
            return ctx.enter_context(nc.sbuf_tensor(name, list(shape), F32R))

        def sem(name):
            return ctx.enter_context(nc.semaphore(name))

        wr_raw, wk_raw, wv_raw = (sb(f"{n}_raw", P, CI, D) for n in ("wr", "wk", "wv"))
        wrT, wkT, wvT = (sbr(f"{n}T", P, 2, CI, D) for n in ("wr", "wk", "wv"))
        w_full = sb("w_full", P, 3, CI, D)
        wo_s = sbr("wo_s", P, 2, CI, D)
        wq_raw = sb("wq_raw", P, CI, D)
        wqG = sb("wqG", P, CI, G, KV)
        wo_p = sb("wo_p", P, CI, D)
        kraw, vraw = sb("kraw", P, CI, KV), sb("vraw", P, CI, KV)
        krawT, vrawT = sb("krawT", KV, CI, P), sb("vrawT", KV, CI, P)
        wc_sb, we_sb, wcT, wce = (sb(n, KV, KV) for n in ("wc_sb", "we_sb", "wcT", "wce"))
        wkv = sb("wkv", P, CI, 2 * KV)
        bkc, bvc = sb("bkc", KV, 1), sb("bvc", KV, 1)
        bk1_rep, bv_rep = sb("bk1_rep", P, KV), sb("bv_rep", P, KV)
        bq1 = sb("bq1", P, G)
        bo_rep, gamma_rep, beta_rep = sb("bo_rep", P, D), sb("gamma_rep", P, D), sb("beta_rep", P, D)
        mur, muk = sb("mur", P, CI), sb("muk", P, CI)
        ident = sb("ident", P, P)
        causal = sb("causal", P, C)
        vmask = sb("vmask", P, J, HD)
        smask = sb("smask", P, J, V1)
        kmask = sb("kmask", P, J)
        spread = sb("spread", P, NC, J, C)
        eps_ln, spacer = sb("eps_ln", P, 2), sb("spacer", P, 1)
        neg_one = sb("neg_one", P, 2)
        neg_half = sb("neg_half", P, 2)

        class Ffn:
            pass

        def ffn_buffers(n):
            f = Ffn()
            f.stats, f.mv = sb(f"{n}_stats", P, 2, 6), sb(f"{n}_mv", P, 2, 2)
            f.veps, f.rstd = sb(f"{n}_veps", P, 2), sb(f"{n}_rstd", P, 2)
            f.negm, f.nmr = sb(f"{n}_negm", P, 2), sb(f"{n}_nmr", P, 2)
            f.h = sb(f"{n}_h", P, 2, D)
            f.hT = sb(f"{n}_hT", P, CI, 2, P + 1)
            f.carry = sb(f"{n}_carry", P, NT + 1, CI, 2)
            f.d = sb(f"{n}_d", P, CI, 2, P)
            f.xk, f.xr = sb(f"{n}_xk", P, CI, 2, P), sb(f"{n}_xr", P, CI, 2, P)
            f.relu, f.ka = sb(f"{n}_relu", P, CI, 2, P), sb(f"{n}_ka", P, CI, 2, P)
            f.xk_s, f.xr_s, f.ka_s = (sbr(f"{n}_{v}_s", P, 2, CI, 2, P) for v in ("xk", "xr", "ka"))
            f.full = {"xk": f.xk, "xr": f.xr, "ka": f.ka}
            f.split = {"xk": f.xk_s, "xr": f.xr_s, "ka": f.ka_s}
            f.th, f.t1 = sb(f"{n}_th", P, 2, D), sb(f"{n}_t1", P, 2, D)
            f.s = {s: sem(f"{n}_{s}_done") for s in
                   ("stats", "mv", "veps", "rstd", "nmr", "h", "hTp", "hT", "edge", "d", "xk", "xr",
                    "xk_hi", "xk_lo", "xr_hi", "xr_lo", "kp", "relu", "ka", "ka_hi", "ka_lo", "rp", "th", "vp",
                    "t1", "y")}
            return f

        f1, f2 = ffn_buffers("f1"), ffn_buffers("f2")
        x_in = sb("x_in", P, NT, 2, D)
        x1 = sb("x1", P, 2, 2, D)
        x2 = sb("x2", P, 2, 2, D)
        x3 = sb("x3", P, 2, 2, D)

        a_stats, a_mv = sb("a_stats", P, 2, 6), sb("a_mv", P, 2, 2)
        a_veps, a_rstd, a_negm, a_nmr = (sb(f"a_{n}", P, 2) for n in ("veps", "rstd", "negm", "nmr"))
        h2 = sb("h2", P, 2, D)
        h2b = sb("h2b", P, 2, 2, D)
        x1b = sb("x1b", P, 2, 2, D)
        h2T = sb("h2T", P, CI, 2, P)
        yk, ek = sb("yk", P, 2, KV), sb("ek", P, 2, KV)
        kf = sb("kf", P, 2, KV)
        vaug = sb("vaug", P, 2, 2, J, V1)
        kbd = sb("kbd", P, NC, J, C)
        yq, eq = sb("yq", P, NC, G, C), sb("eq", P, NC, G, C)
        qf = sb("qf", P, 2, NC, G, C)
        vbd = sb("vbd", P, 2, NC, J, V1)
        am = sb("am", P, 2, NC, G, C)
        sp = sb("sp", P, NC, VW)
        st = sb("st", P, 2, NC, VW)
        st_carry = sb("st_carry", P, NT + 1, VW)
        den, rden = sb("den", P, 2, J * G), sb("rden", P, 2, J * G)
        attn = sb("attn", P, 2, NC, KV)
        attnT_s = sbr("attnT_s", P, 2, CI, 2, P)
        y = sb("y", P, 2, D)
        y_stats, y_mv = sb("y_stats", P, 2, 6), sb("y_mv", P, 2, 2)
        y_veps, y_rstd = sb("y_veps", P, 2), sb("y_rstd", P, 2)
        z = sb("z", P, 2, D)

        def psum(name):
            return ctx.enter_context(nc.psum_tensor(name, [P, 512], F32))

        bank_T, bank_K, bank_R, bank_V, bank_Q, bank_KV, bank_0, bank_1 = (
            psum(n) for n in ("bank_T", "bank_K", "bank_R", "bank_V", "bank_Q", "bank_KV", "bank_0", "bank_1"))
        psT = bank_T[:, :].rearrange("q (c p t) -> q c p t", c=CI, p=2)
        psK = bank_K[:, :].rearrange("q (c n) -> q c n", c=CI)
        psR = bank_R[:, :].rearrange("q (p d) -> q p d", p=2)
        psV = bank_V[:, :].rearrange("q (p d) -> q p d", p=2)
        psQ = bank_Q[:, :].rearrange("q (g t) -> q g t", g=G)
        psKV = bank_KV[:, 0:4 * KV].rearrange("q (p n) -> q p n", p=2)
        psKT = bank_KV[:, 4 * KV:4 * KV + P]
        psS = bank_KV[:, 0:NC * VW].rearrange("q (c n) -> q c n", c=NC)
        psO = [b[:, 0:NC * VW].rearrange("q (c j d) -> q c j d", c=NC, j=J) for b in (bank_Q, bank_KV)]
        psVB = bank_0[:, :].rearrange("q (c p n) -> q c p n", c=NC, p=2)
        psA = [b[:, :].rearrange("q (c g t) -> q c g t", c=NC, g=G) for b in (bank_0, bank_1)]
        psOT = bank_1[:, :].rearrange("q (c p t) -> q c p t", c=CI, p=2)
        psW = bank_1[:, :].rearrange("q (p d) -> q p d", p=2)

        w_loaded = sem("w_loaded")
        x_loaded, stored = [sem("x_loaded0"), sem("x_loaded1")], [sem("stored0"), sem("stored1")]
        consts = sem("consts")
        mask_step = sem("mask_step")
        setup_pe, setup_dve = sem("setup_pe"), sem("setup_dve")
        A = {n: sem(f"a_{n}_done") for n in (
            "stats", "mv", "veps", "rstd", "nmr", "h", "hTp", "hT", "h2b", "x1b", "kvp", "qp", "yk", "vaug",
            "ek", "kf", "kTp", "kbd", "yq", "eq", "qf", "vbp", "vb", "Sp", "sp",
            "st0", "st", "stc", "A0p", "A1p", "A0", "A1", "O0p", "O1p", "den0", "den1", "rden0", "rden1",
            "o0", "o1", "oTp", "oT_hi", "oT_lo", "wp", "y", "ystats", "ymv", "yveps", "yrstd", "z", "x2")}

        x_dram = x.rearrange("(p b) (n t) c -> b n t p c", p=2, t=P)
        out_dram = out.rearrange("(p b) (n t) c -> b n t p c", p=2, t=P)
        loads = []

        def row(v):
            return v.rearrange("(a c) -> a c", a=1)

        for dst, src in ((wr_raw, W_r), (wk_raw, W_k), (wv_raw, W_v), (wq_raw, Wq), (kraw, Wk), (vraw, Wv)):
            loads.append((dst[:], src.rearrange("(o q) c -> q o c", q=P)))
        for dst, src in ((wc_sb, Wc), (we_sb, We)):
            loads.append((dst[:], src))
        for g in range(G):
            for j in range(J):
                q0 = (g % 2) * KV + j * HD
                loads.append((wo_p[q0:q0 + HD, g // 2, :], Wo[(j * G + g) * HD:(j * G + g + 1) * HD, :]))
        for dst, src in ((bkc, bk), (bvc, bv)):
            loads.append((dst[:], src.rearrange("(q a) -> q a", a=1)))
        for p in range(2):
            for j in range(J):
                q0 = p * KV + j * HD
                loads.append((bq1[q0:q0 + HD, :],
                              bq.rearrange("(j g f) -> j f g", j=J, g=G)[j]))
        for dst, src in ((bo_rep, bo), (gamma_rep, gamma), (beta_rep, beta)):
            loads.append((dst[:], row(src).broadcast_to([P, D])))
        for dst, src in ((mur, mu_r), (muk, mu_k)):
            loads.append((dst[:], src.rearrange("(c q) -> q c", q=P)))
        W_ALL = 16 * len(loads)

        LAST = STEPS - 1
        MAX_LAG = 5
        FIRST = MAX_LAG + 1

        def run(eng, body):
            def iteration(i, u):
                def stage(work, lag, *args):
                    if has(i - lag):
                        work(i - lag, (u - lag) % 2, *args)
                body(stage)

            for i in range(FIRST):
                iteration(i, i % 2)
            with eng.Fori(FIRST // 2, STEPS // 2) as m:
                for u in range(2):
                    iteration(m * 2 + u, u)
            for i in range(STEPS, STEPS + MAX_LAG + 1):
                iteration(i, i % 2)

        def has(k):
            return not isinstance(k, int) or 0 <= k <= LAST

        def upto(k):
            return min(k, LAST) + 1 if isinstance(k, int) else k + 1

        block = ctx.enter_context(nc.Block())

        @block.sync
        def _(sp_eng):
            def load(k, q):
                sp_eng.dma_start(x_in[:, k % NT], x_dram[k // NT, k % NT]).then_inc(x_loaded[q], 16)

            load(0, 0)
            for dst, src in loads:
                sp_eng.dma_start(dst, src, allow_slow_non_contiguous=True).then_inc(w_loaded, 16)
            load(1, 1)

            def load_next(k, q):
                if has(k - 2):
                    sp_eng.wait_ge(f1.s["stats"], upto(k - 2))
                    load(k, q)

            def store(k, q):
                sp_eng.wait_ge(f2.s["y"], upto(k))
                sp_eng.dma_start(out_dram[k // NT, k % NT], x3[:, q]).then_inc(stored[q], 16)

            def body(stage):
                stage(load_next, 0)
                stage(store, 5)

            run(sp_eng, body)
            for u in range(2):
                sp_eng.wait_ge(stored[u], 16 * (STEPS // 2))

        @block.tensor
        def _(pe):
            mm, tr = nc.tensor.matmul, nc.tensor.transpose

            pe.wait_ge(consts, 1)
            pe.wait_ge(w_loaded, W_ALL)
            for raw, bank in ((wr_raw, bank_T), (wk_raw, bank_K), (wv_raw, bank_R)):
                for ci in range(CI):
                    for do in range(CI):
                        last = tr(bank[:, ci * D + do * P:ci * D + (do + 1) * P],
                                  raw[:, do, ci * P:(ci + 1) * P], ident[:])
                last.then_inc(setup_pe, 1)
            for raw, bank in ((kraw, bank_V), (vraw, bank_Q)):
                for ci in range(CI):
                    last = tr(bank[0:KV, ci * P:(ci + 1) * P], raw[:, ci, :], ident[:])
                last.then_inc(setup_pe, 1)
            tr(bank_KV[0:KV, 0:KV], wc_sb[:], ident[0:KV, 0:KV]).then_inc(setup_pe, 1)
            pe.wait_ge(setup_dve, 6)
            mm(bank_0[0:KV, 0:KV], wcT[:], we_sb[:], start=True, stop=True).then_inc(setup_pe, 1)
            pe.wait_ge(setup_dve, 7)
            for ci in range(CI):
                for n, t in enumerate((krawT, vrawT)):
                    o = ci * 2 * KV + n * KV
                    last = mm(bank_1[:, o:o + KV], t[:, ci, :], wce[:], start=True, stop=True)
            last.then_inc(setup_pe, 1)
            for n, b in enumerate((bkc, bvc)):
                last = mm(bank_KV[:, n * KV:(n + 1) * KV], b[:].broadcast_to([KV, P]), wce[:],
                          start=True, stop=True)
            last.then_inc(setup_pe, 1)
            pe.wait_ge(setup_dve, 17)

            def products(out_of, lhs_of, rhs_of):
                terms = [(hl, hr, ci) for hl, hr in ((0, 0), (0, 1), (1, 0)) for ci in range(CI)]
                for n, (hl, hr, ci) in enumerate(terms):
                    last = mm(out_of, lhs_of(hl, ci), rhs_of(hr, ci), start=n == 0, stop=n == len(terms) - 1)
                return last

            def bank_free(evacuated, k):
                if has(k):
                    pe.wait_ge(evacuated, upto(k))

            def transposes(ps, src, done):
                for p in range(2):
                    for ci in range(CI):
                        last = tr(ps[:, ci, p, :], src[:, p, ci * P:(ci + 1) * P], ident[:])
                last.then_inc(done, 1)

            def ffn_T1(k, q):
                pe.wait_ge(f1.s["h"], upto(k))
                bank_free(A["hT"], k - 2)
                transposes(psT, f1.h, f1.s["hTp"])

            def ffn_T2(k, q):
                pe.wait_ge(f2.s["h"], upto(k))
                bank_free(f1.s["hT"], k + 3)
                transposes(psT, f2.h, f2.s["hTp"])

            def ffn_K(k, q, f, other, other_k):
                pe.wait_ge(f.s["xk_hi"], upto(k))
                pe.wait_ge(f.s["xk_lo"], upto(k))
                bank_free(other.s["relu"], k + other_k)
                for co in range(CI):
                    last = products(psK[:, co, :], lambda h, ci: wkT[:, h, ci, co * P:(co + 1) * P],
                                    lambda h, ci: f.xk_s[:, h, ci].rearrange("q p t -> q (p t)"))
                last.then_inc(f.s["kp"], 1)

            def ffn_R(k, q, f, other, other_k):
                pe.wait_ge(f.s["xr_hi"], upto(k))
                pe.wait_ge(f.s["xr_lo"], upto(k))
                bank_free(other.s["th"], k + other_k)
                for p in range(2):
                    last = products(psR[:, p, :], lambda h, ci: f.xr_s[:, h, ci, p, :], lambda h, ci: wrT[:, h, ci, :])
                last.then_inc(f.s["rp"], 1)

            def ffn_V(k, q, f, other, other_k):
                pe.wait_ge(f.s["ka_hi"], upto(k))
                pe.wait_ge(f.s["ka_lo"], upto(k))
                bank_free(other.s["t1"], k + other_k)
                for p in range(2):
                    last = products(psV[:, p, :], lambda h, ci: f.ka_s[:, h, ci, p, :], lambda h, ci: wvT[:, h, ci, :])
                last.then_inc(f.s["vp"], 1)

            def attn_T(k, q):
                pe.wait_ge(A["h"], upto(k))
                bank_free(f2.s["hT"], k - 2)
                transposes(psT, h2, A["hTp"])

            def kv_product(k, q):
                pe.wait_ge(A["hT"], upto(k))
                bank_free(A["o1"], k - 1)
                for p in range(2):
                    for ci in range(CI):
                        last = mm(psKV[:, p, :], h2T[:, ci, p, :], wkv[:, ci, :], start=ci == 0, stop=ci == CI - 1)
                last.then_inc(A["kvp"], 1)

            def q_product(k, q):
                bank_free(A["o0"], k - 1)
                for g in range(G):
                    for ci in range(CI):
                        for p in range(2):
                            last = mm(psQ[p * KV:(p + 1) * KV, g, :], wqG[:, ci, g, :], h2T[:, ci, p, :],
                                      start=ci == 0, stop=ci == CI - 1)
                last.then_inc(A["qp"], 1)

            def k_transpose(k, q):
                pe.wait_ge(A["kf"], upto(k))
                tr(psKT, kf[:].rearrange("q p n -> q (p n)"), ident[:]).then_inc(A["kTp"], 1)

            def v_spread(k, q):
                pe.wait_ge(A["vaug"], upto(k))
                bank_free(A["A0"], k - 1)
                for n in range(NC):
                    last = mm(psVB[:, n].rearrange("q p (j d) -> q p j d", j=J),
                              spread[:, n].rearrange("q j s -> q (j s)"),
                              vaug[:, q, :, :, 0:HD], start=True, stop=True)
                last.then_inc(A["vbp"], 1)

            def state_growth(k, q):
                pe.wait_ge(A["kbd"], upto(k))
                for n in range(NC):
                    for p in range(2):
                        last = mm(psS[p * KV:(p + 1) * KV, n, :], kf[0:(n + 1) * C, p, :],
                                  vaug[0:(n + 1) * C, q, p].rearrange("q j d -> q (j d)"),
                                  start=True, stop=True)
                last.then_inc(A["Sp"], 1)

            def scores(k, q, p):
                pe.wait_ge(A["qf"], upto(k))
                pe.wait_ge(A["kbd"], upto(k))
                if p == 0:
                    pe.wait_ge(A["vb"], upto(k))
                else:
                    bank_free(A["y"], k - 1)
                for n in range(NC):
                    last = mm(psA[p][:, n].rearrange("q g t -> q (g t)"),
                              kbd[p * KV:(p + 1) * KV, n].rearrange("q j s -> q (j s)"),
                              qf[p * KV:(p + 1) * KV, q, n].rearrange("q g t -> q (g t)"), start=True, stop=True)
                last.then_inc(A[f"A{p}p"], 1)

            def attend(k, q, p):
                pe.wait_ge(A[f"A{p}"], upto(k))
                pe.wait_ge(A["vb"], upto(k))
                pe.wait_ge(A["st"], upto(k))
                for n in range(NC):
                    ps = psO[p][:, n].rearrange("q j d -> q (j d)")
                    mm(ps, am[:, p, n].rearrange("q g t -> q (g t)"), vbd[:, p, n].rearrange("q j d -> q (j d)"),
                       start=True, stop=False)
                    last = mm(ps, qf[p * KV:(p + 1) * KV, q, n].rearrange("q g t -> q (g t)"),
                              st[p * KV:(p + 1) * KV, q, n, :], start=False, stop=True)
                last.then_inc(A[f"O{p}p"], 1)

            def output_transpose(k, q):
                for p in range(2):
                    pe.wait_ge(A[f"o{p}"], upto(k))
                pe.wait_ge(A["A1"], upto(k))
                pick = ident[:].rearrange("q (gc gp t) -> q gc gp t", gc=CI, gp=2)
                for p in range(2):
                    for n in range(NC):
                        for gp in range(2):
                            last = mm(psOT[gp * KV:(gp + 1) * KV, :, p, n * C:(n + 1) * C], attn[:, p, n, :],
                                      pick[:, :, gp, :], start=True, stop=True)
                last.then_inc(A["oTp"], 1)

            def output_product(k, q):
                pe.wait_ge(A["oT_hi"], upto(k))
                pe.wait_ge(A["oT_lo"], upto(k))
                for p in range(2):
                    last = products(psW[:, p, :], lambda h, ci: attnT_s[:, h, ci, p, :], lambda h, ci: wo_s[:, h, ci, :])
                last.then_inc(A["wp"], 1)

            def body(stage):
                stage(ffn_K, 1, f1, f2, -3)
                stage(output_product, 3)
                stage(attn_T, 2)
                stage(ffn_R, 4, f2, f1, 2)
                stage(kv_product, 2)
                stage(q_product, 2)
                stage(k_transpose, 2)
                stage(v_spread, 2)
                stage(ffn_T1, 0)
                stage(ffn_V, 4, f2, f1, 2)
                stage(state_growth, 2)
                stage(scores, 2, 1)
                stage(ffn_T2, 3)
                stage(scores, 2, 0)
                stage(ffn_R, 1, f1, f2, -3)
                stage(ffn_V, 1, f1, f2, -3)
                stage(attend, 2, 0)
                stage(attend, 2, 1)
                stage(ffn_K, 3, f2, f1, 2)
                stage(output_transpose, 2)

            run(pe, body)

        @block.scalar
        def _(act):
            activation = nc.scalar.activation

            def normalise(s, k, dst, src, rstd, nmr):
                act.wait_ge(s["nmr"], upto(k))
                for p in range(2):
                    last = activation(dst[:, p, :], src[:, p, :], ACT.Identity, bias=nmr[:, p:p + 1],
                                      scale=rstd[:, p:p + 1])
                last.then_inc(s["h"], 1)

            def normalise_x(k, q):
                normalise(f1.s, k, f1.h, x_in[:, k % NT], f1.rstd, f1.nmr)

            def normalise_x1(k, q):
                normalise(A, k, h2, x1[:, q], a_rstd, a_nmr)

            def normalise_x2(k, q):
                normalise(f2.s, k, f2.h, x2[:, q], f2.rstd, f2.nmr)

            def evacuate_hT(k, q, f):
                act.wait_ge(f.s["hTp"], upto(k))
                activation(f.hT[:, :, :, 1:], psT, ACT.Copy).then_inc(f.s["hT"], 1)

            def evacuate_h2T(k, q):
                act.wait_ge(A["hTp"], upto(k))
                activation(h2T[:], psT, ACT.Copy).then_inc(A["hT"], 1)

            def high(k, q, f, name):
                act.wait_ge(f.s[name], upto(k))
                activation(f.split[name][:, 0], f.full[name][:], ACT.Copy).then_inc(f.s[f"{name}_hi"], 1)

            def k_relu(k, q, f):
                act.wait_ge(f.s["kp"], upto(k))
                activation(f.relu[:].rearrange("q c p t -> q (c p t)"), bank_K[:, :], ACT.Relu).then_inc(f.s["relu"], 1)

            def k_square(k, q, f):
                act.wait_ge(f.s["relu"], upto(k))
                activation(f.ka[:], f.relu[:], ACT.Square).then_inc(f.s["ka"], 1)

            def r_tanh(k, q, f):
                act.wait_ge(f.s["rp"], upto(k))
                activation(f.th[:], psR, ACT.Tanh, scale=0.5).then_inc(f.s["th"], 1)

            def exp_k(k, q):
                act.wait_ge(A["yk"], upto(k))
                activation(ek[:], yk[:], ACT.Exp, bias=-1.0).then_inc(A["ek"], 1)

            def exp_q(k, q):
                act.wait_ge(A["yq"], upto(k))
                activation(eq[:], yq[:], ACT.Exp, bias=-1.0).then_inc(A["eq"], 1)

            def block_diagonal_k(k, q):
                act.wait_ge(A["kTp"], upto(k))
                for j in range(J):
                    last = activation(kbd[:, :, j, :], psKT.rearrange("q (c s) -> q c s", c=NC), ACT.Identity,
                                      scale=kmask[:, j:j + 1])
                last.then_inc(A["kbd"], 1)

            def output_high(k, q):
                act.wait_ge(A["oTp"], upto(k))
                activation(attnT_s[:, 0], psOT, ACT.Copy).then_inc(A["oT_hi"], 1)

            def body(stage):
                stage(k_square, 4, f2)
                stage(high, 4, f2, "ka")
                stage(evacuate_h2T, 2)
                stage(k_relu, 1, f1)
                stage(normalise_x, 0)
                stage(high, 1, f1, "xr")
                stage(exp_k, 2)
                stage(k_square, 1, f1)
                stage(high, 1, f1, "ka")
                stage(block_diagonal_k, 2)
                stage(exp_q, 2)
                stage(evacuate_hT, 0, f1)
                stage(r_tanh, 4, f2)
                stage(normalise_x2, 3)
                stage(evacuate_hT, 3, f2)
                stage(high, 3, f2, "xk")
                stage(r_tanh, 1, f1)
                stage(high, 0, f1, "xk")
                stage(k_relu, 3, f2)
                stage(output_high, 2)
                stage(high, 3, f2, "xr")
                stage(normalise_x1, 1)

            run(act, body)

        @block.vector
        def _(dve):
            v = nc.vector

            for n, (bank, factor) in enumerate(((bank_T, 1.0), (bank_K, 1.0), (bank_R, 0.25))):
                dve.wait_ge(setup_pe, n + 1)
                v.tensor_scalar(w_full[:, n].rearrange("q c d -> q (c d)"), bank[:, :], factor, None,
                                ALU.mult).then_inc(setup_dve, 1)
            for n, (t, bank) in enumerate(((krawT, bank_V), (vrawT, bank_Q))):
                dve.wait_ge(setup_pe, 4 + n)
                v.tensor_copy(t[:].rearrange("q c d -> q (c d)"), bank[0:KV, 0:CI * P]).then_inc(setup_dve, 1)
            dve.wait_ge(setup_pe, 6)
            v.tensor_copy(wcT[:], bank_KV[0:KV, 0:KV]).then_inc(setup_dve, 1)
            dve.wait_ge(setup_pe, 7)
            v.tensor_copy(wce[:], bank_0[0:KV, 0:KV]).then_inc(setup_dve, 1)
            dve.wait_ge(setup_pe, 8)
            v.tensor_copy(wkv[:].rearrange("q c d -> q (c d)"), bank_1[:, 0:CI * 2 * KV]).then_inc(setup_dve, 1)
            dve.wait_ge(setup_pe, 9)
            v.tensor_scalar(bk1_rep[:], bank_KV[:, 0:KV], 1.0, None, ALU.add).then_inc(setup_dve, 1)
            v.tensor_copy(bv_rep[:], bank_KV[:, KV:2 * KV]).then_inc(setup_dve, 1)
            for ci in range(CI):
                v.tensor_copy(wqG[:, ci], wq_raw[:, ci].rearrange("q (j g f) -> q g j f", j=J, g=G)).then_inc(setup_dve, 1)
            v.tensor_scalar(bq1[:], bq1[:], 1.0, None, ALU.add).then_inc(setup_dve, 1)
            dve.wait_ge(consts, 2)
            v.tensor_copy(vbd[:, :, :, :, HD].rearrange("q p c j -> q (p c) j"),
                          vmask[:, :, 0].unsqueeze(1).broadcast_to([P, 2 * NC, J])).then_inc(setup_dve, 1)
            v.tensor_copy(spread[:], ident[:].rearrange("q (c s) -> q c s", c=NC).unsqueeze(2)
                          .broadcast_to([P, NC, J, C])).then_inc(setup_dve, 1)
            dve.wait_ge(setup_dve, 15)
            for split, full in ((wrT, w_full[:, 0]), (wkT, w_full[:, 1]), (wvT, w_full[:, 2]), (wo_s, wo_p[:])):
                last = v.tensor_copy(split[:, 0], full)
            last.then_inc(setup_dve, 1)
            dve.wait_ge(setup_dve, 16)
            for split, full in ((wrT, w_full[:, 0]), (wkT, w_full[:, 1]), (wvT, w_full[:, 2]), (wo_s, wo_p[:])):
                last = v.tensor_tensor(split[:, 1], full, split[:, 0].bitcast(F32), ALU.subtract)
            last.then_inc(setup_dve, 1)
            dve.wait_ge(setup_dve, 17)

            def statistics(src, stats, mv, s, stats_name, mv_name, k):
                for p in range(2):
                    last = v.bn_stats(stats[:, p, :], src[:, p, :])
                last.then_inc(s[stats_name], 1)
                dve.wait_ge(s[stats_name], upto(k))
                v.memset(spacer[:], 0.0)
                for p in range(2):
                    last = v.bn_aggr(mv[:, p, :], stats[:, p, :])
                last.then_inc(s[mv_name], 1)

            def x_statistics(k, q):
                dve.wait_ge(x_loaded[q], 16 * (k // 2 + 1))
                statistics(x_in[:, k % NT], f1.stats, f1.mv, f1.s, "stats", "mv", k)

            def x1_statistics(k, q):
                dve.wait_ge(f1.s["y"], upto(k))
                statistics(x1[:, q], a_stats, a_mv, A, "stats", "mv", k)

            def x2_statistics(k, q):
                dve.wait_ge(A["x2"], upto(k))
                statistics(x2[:, q], f2.stats, f2.mv, f2.s, "stats", "mv", k)

            def difference(k, q, f):
                n = k % NT
                dve.wait_ge(f.s["hT"], upto(k))
                v.tensor_copy(f.hT[:, :, :, 0], f.carry[:, n]).then_inc(f.s["edge"], 1)
                v.tensor_copy(f.carry[:, n + 1], f.hT[:, :, :, P])
                dve.wait_ge(f.s["edge"], upto(k))
                v.tensor_tensor(f.d[:], f.hT[:, :, :, 1:], f.hT[:, :, :, 0:P], ALU.subtract).then_inc(f.s["d"], 1)

            def mix(k, q, f, name, mu):
                dve.wait_ge(f.s["d"], upto(k))
                for ci in range(CI):
                    last = v.scalar_tensor_tensor(out=f.full[name][:, ci], in0=f.d[:, ci], scalar=mu[:, ci:ci + 1],
                                                  in1=f.hT[:, ci, :, 0:P], op0=ALU.mult, op1=ALU.add)
                last.then_inc(f.s[name], 1)

            def low(k, q, f, name):
                dve.wait_ge(f.s[f"{name}_hi"], upto(k))
                v.tensor_tensor(f.split[name][:, 1], f.full[name][:], f.split[name][:, 0].bitcast(F32),
                                ALU.subtract).then_inc(f.s[f"{name}_lo"], 1)

            def gate(k, q, f):
                dve.wait_ge(f.s["th"], upto(k))
                dve.wait_ge(f.s["vp"], upto(k))
                v.scalar_tensor_tensor(out=f.t1[:], in0=f.th[:], scalar=1.0, in1=psV, op0=ALU.add,
                                       op1=ALU.mult).then_inc(f.s["t1"], 1)

            def k_bias(k, q):
                dve.wait_ge(A["kvp"], upto(k))
                v.tensor_tensor(yk[:], psKV[:, :, 0:KV], bk1_rep[:].unsqueeze(1).broadcast_to([P, 2, KV]),
                                ALU.add).then_inc(A["yk"], 1)

            def v_bias(k, q):
                dve.wait_ge(A["kvp"], upto(k))
                for p in range(2):
                    last = v.tensor_tensor(vaug[:, q, p, :, 0:HD],
                                           psKV[:, p, KV:2 * KV].rearrange("q (j d) -> q j d", j=J),
                                           bv_rep[:].rearrange("q (j d) -> q j d", j=J), ALU.add)
                last.then_inc(A["vaug"], 1)

            def q_bias(k, q):
                dve.wait_ge(A["qp"], upto(k))
                v.tensor_tensor(yq[:].rearrange("q c g t -> q g c t"), psQ.rearrange("q g (c t) -> q g c t", c=NC),
                                bq1[:].unsqueeze(2).unsqueeze(3).broadcast_to([P, G, NC, C]),
                                ALU.add).then_inc(A["yq"], 1)

            def k_feature(k, q):
                dve.wait_ge(A["ek"], upto(k))
                v.scalar_tensor_tensor(out=kf[:], in0=yk[:], scalar=1.0, in1=ek[:], op0=ALU.max,
                                       op1=ALU.min).then_inc(A["kf"], 1)

            def q_feature(k, q):
                dve.wait_ge(A["eq"], upto(k))
                v.scalar_tensor_tensor(out=qf[:, q], in0=yq[:], scalar=1.0, in1=eq[:], op0=ALU.max,
                                       op1=ALU.min).then_inc(A["qf"], 1)

            def block_diagonal_v(k, q):
                dve.wait_ge(A["vbp"], upto(k))
                for p in range(2):
                    last = v.tensor_tensor(vbd[:, p, :, :, 0:HD], psVB[:, :, p].rearrange("q c (j d) -> q c j d", j=J),
                                           vmask[:].unsqueeze(1).broadcast_to([P, NC, J, HD]), ALU.mult)
                last.then_inc(A["vb"], 1)

            def mask_state(k, q):
                dve.wait_ge(A["Sp"], upto(k))
                v.tensor_tensor(sp[:], psS,
                                smask[:].rearrange("q j d -> q (j d)").unsqueeze(1).broadcast_to([P, NC, VW]),
                                ALU.mult).then_inc(A["sp"], 1)

            def causal_mask(k, q, p):
                dve.wait_ge(A[f"A{p}p"], upto(k))
                v.tensor_tensor(am[:, p].rearrange("q c g t -> q (c g) t"), psA[p].rearrange("q c g t -> q (c g) t"),
                                causal[:].unsqueeze(1).broadcast_to([P, NC * G, C]), ALU.mult).then_inc(A[f"A{p}"], 1)

            def normalise_output(k, q, p):
                dve.wait_ge(A[f"O{p}p"], upto(k))
                v.tensor_scalar(den[:, p].rearrange("q (c j) -> q c j", c=NC), psO[p][:, :, :, HD], EPS_DEN, None,
                                ALU.add).then_inc(A[f"den{p}"], 1)
                dve.wait_ge(A[f"den{p}"], upto(k))
                v.reciprocal(rden[:, p], den[:, p]).then_inc(A[f"rden{p}"], 1)
                dve.wait_ge(A[f"rden{p}"], upto(k))
                v.tensor_tensor(attn[:, p].rearrange("q c (j d) -> q (c j) d", j=J),
                                psO[p].rearrange("q c j d -> q (c j) d")[:, :, 0:HD],
                                rden[:, p].unsqueeze(2).broadcast_to([P, NC * J, HD]),
                                ALU.mult).then_inc(A[f"o{p}"], 1)

            def output_low(k, q):
                dve.wait_ge(A["oT_hi"], upto(k))
                v.tensor_tensor(attnT_s[:, 1], psOT, attnT_s[:, 0].bitcast(F32), ALU.subtract).then_inc(A["oT_lo"], 1)

            def attention_residual(k, q):
                dve.wait_ge(A["h2b"], upto(k))
                dve.wait_ge(A["wp"], upto(k))
                v.tensor_tensor(y[:], psW, h2b[:, q], ALU.add).then_inc(A["y"], 1)

            def y_statistics(k, q):
                dve.wait_ge(A["y"], upto(k))
                statistics(y, y_stats, y_mv, A, "ystats", "ymv", k)

            def centre_y(k, q):
                dve.wait_ge(A["ymv"], upto(k))
                for p in range(2):
                    last = v.scalar_tensor_tensor(out=z[:, p], in0=y[:, p], scalar=y_mv[:, p, 0:1],
                                                  in1=gamma_rep[:], op0=ALU.subtract, op1=ALU.mult)
                last.then_inc(A["z"], 1)

            def x2_sum(k, q):
                dve.wait_ge(A["yrstd"], upto(k))
                dve.wait_ge(A["x1b"], upto(k))
                dve.wait_ge(A["z"], upto(k))
                for p in range(2):
                    last = v.scalar_tensor_tensor(out=x2[:, q, p], in0=z[:, p], scalar=y_rstd[:, p:p + 1],
                                                  in1=x1b[:, q, p], op0=ALU.mult, op1=ALU.add)
                last.then_inc(A["x2"], 1)

            def body(stage):
                stage(block_diagonal_v, 3)
                stage(q_feature, 3)
                stage(gate, 5, f2)
                stage(causal_mask, 3, 1)
                stage(mask_state, 3)
                stage(difference, 4, f2)
                stage(mix, 4, f2, "xk", muk)
                stage(causal_mask, 3, 0)
                stage(mix, 1, f1, "xk", muk)
                stage(gate, 2, f1)
                stage(normalise_output, 3, 0)
                stage(normalise_output, 3, 1)
                stage(x1_statistics, 2)
                stage(mix, 4, f2, "xr", mur)
                stage(output_low, 3)
                stage(x_statistics, 0)
                stage(mix, 1, f1, "xr", mur)
                stage(attention_residual, 3)
                stage(y_statistics, 3)
                stage(centre_y, 3)
                stage(v_bias, 2)
                stage(k_bias, 2)
                stage(x2_sum, 3)
                stage(k_feature, 2)
                stage(x2_statistics, 3)
                stage(q_bias, 2)
                stage(low, 1, f1, "xr")

            run(dve, body)

        @block.gpsimd
        def _(pool):
            g_ = nc.gpsimd

            count = [0]

            def in_turn(ins):
                count[0] += 1
                ins.then_inc(mask_step, 1)
                pool.wait_ge(mask_step, count[0])

            def keep(t, base, pattern, channel):
                in_turn(g_.affine_select(out=t, in_=t, compare_op=ALU.is_ge, fill=0.0, base=base, pattern=pattern,
                                         channel_multiplier=channel))

            in_turn(g_.memset(ident[:], 0.0))
            g_.affine_select(out=ident[:], in_=ident[:], compare_op=ALU.not_equal, fill=1.0, base=0,
                             pattern=[[-1, P]], channel_multiplier=1).then_inc(consts, 1)
            for t in (causal, vmask, smask, kmask):
                in_turn(g_.memset(t[:], 1.0))
            for j in range(J):
                keep(causal[j * C:(j + 1) * C], 0, [[1, C]], -1)
            keep(vmask[:], 0, [[-C, J], [0, HD]], 1)
            keep(vmask[:], C - 1, [[C, J], [0, HD]], -1)
            for p in range(2):
                q = slice(p * KV, (p + 1) * KV)
                keep(smask[q], 0, [[-HD, J], [0, V1]], 1)
                keep(smask[q], HD - 1, [[HD, J], [0, V1]], -1)
                keep(kmask[q], 0, [[-HD, J]], 1)
                keep(kmask[q], HD - 1, [[HD, J]], -1)
            for f in (f1, f2):
                in_turn(g_.memset(f.carry[:, 0], 0.0))
            in_turn(g_.memset(st_carry[:, 0], 0.0))
            in_turn(g_.memset(eps_ln[:], EPS_LN))
            in_turn(g_.memset(neg_one[:], -1.0))
            in_turn(g_.memset(neg_half[:], -0.5))
            g_.memset(vaug[:, :, :, :, HD:], 1.0).then_inc(consts, 1)
            pool.wait_ge(consts, 2)
            pool.wait_ge(w_loaded, W_ALL)

            def inverse_deviation(s, names, mv, veps, rstd, k):
                g_.tensor_tensor(veps[:], mv[:, :, 1], eps_ln[:], ALU.add).then_inc(s[names[0]], 1)
                pool.wait_ge(s[names[0]], upto(k))
                g_.tensor_tensor(rstd[:], veps[:], neg_half[:], ALU.pow).then_inc(s[names[1]], 1)

            def norm_factors(s, mv, veps, rstd, negm, nmr, k):
                pool.wait_ge(s["mv"], upto(k))
                g_.tensor_tensor(negm[:], mv[:, :, 0], neg_one[:], ALU.mult)
                inverse_deviation(s, ("veps", "rstd"), mv, veps, rstd, k)
                pool.wait_ge(s["rstd"], upto(k))
                g_.tensor_tensor(nmr[:], negm[:], rstd[:], ALU.mult).then_inc(s["nmr"], 1)

            def x_factors(k, q):
                norm_factors(f1.s, f1.mv, f1.veps, f1.rstd, f1.negm, f1.nmr, k)

            def x1_factors(k, q):
                norm_factors(A, a_mv, a_veps, a_rstd, a_negm, a_nmr, k)

            def x2_factors(k, q):
                norm_factors(f2.s, f2.mv, f2.veps, f2.rstd, f2.negm, f2.nmr, k)

            def y_factors(k, q):
                pool.wait_ge(A["ymv"], upto(k))
                inverse_deviation(A, ("yveps", "yrstd"), y_mv, y_veps, y_rstd, k)

            def difference(k, q, f):
                n = k % NT
                pool.wait_ge(f.s["hT"], upto(k))
                g_.tensor_copy(f.hT[:, :, :, 0], f.carry[:, n]).then_inc(f.s["edge"], 1)
                g_.tensor_copy(f.carry[:, n + 1], f.hT[:, :, :, P])
                pool.wait_ge(f.s["edge"], upto(k))
                g_.tensor_tensor(f.d[:], f.hT[:, :, :, 1:], f.hT[:, :, :, 0:P], ALU.subtract).then_inc(f.s["d"], 1)

            def low(k, q, f, name):
                pool.wait_ge(f.s[f"{name}_hi"], upto(k))
                g_.tensor_tensor(f.split[name][:, 1], f.full[name][:], f.split[name][:, 0].bitcast(F32),
                                 ALU.subtract).then_inc(f.s[f"{name}_lo"], 1)

            def x1_sum(k, q):
                pool.wait_ge(f1.s["t1"], upto(k))
                g_.tensor_tensor(x1[:, q], x_in[:, k % NT], f1.t1[:], ALU.add).then_inc(f1.s["y"], 1)

            def x3_sum(k, q):
                if has(k - 2):
                    pool.wait_ge(stored[q], 16 * (k // 2))
                pool.wait_ge(f2.s["t1"], upto(k))
                g_.tensor_tensor(x3[:, q], x2[:, q], f2.t1[:], ALU.add).then_inc(f2.s["y"], 1)

            def h2_and_bo(k, q):
                pool.wait_ge(A["h"], upto(k))
                g_.tensor_tensor(h2b[:, q], h2[:], bo_rep[:].unsqueeze(1).broadcast_to([P, 2, D]),
                                 ALU.add).then_inc(A["h2b"], 1)

            def x1_and_beta(k, q):
                pool.wait_ge(f1.s["y"], upto(k))
                g_.tensor_tensor(x1b[:, q], x1[:, q], beta_rep[:].unsqueeze(1).broadcast_to([P, 2, D]),
                                 ALU.add).then_inc(A["x1b"], 1)

            def states(k, q):
                n = k % NT
                g_.tensor_copy(st[:, q, 0], st_carry[:, n]).then_inc(A["st0"], 1)
                pool.wait_ge(A["sp"], upto(k))
                pool.wait_ge(A["st0"], upto(k))
                g_.tensor_tensor(st[:, q, 1:], sp[:, 0:NC - 1],
                                 st[:, q, 0].unsqueeze(1).broadcast_to([P, NC - 1, VW]),
                                 ALU.add).then_inc(A["st"], 1)
                g_.tensor_tensor(st_carry[:, n + 1], sp[:, NC - 1], st[:, q, 0], ALU.add).then_inc(A["stc"], 1)

            def body(stage):
                stage(low, 5, f2, "xr")
                stage(x_factors, 1)
                stage(x1_and_beta, 4)
                stage(y_factors, 4)
                stage(low, 5, f2, "ka")
                stage(h2_and_bo, 3)
                stage(x2_factors, 4)
                stage(low, 2, f1, "ka")
                stage(difference, 1, f1)
                stage(x3_sum, 5)
                stage(states, 3)
                stage(low, 4, f2, "xk")
                stage(x1_sum, 2)
                stage(low, 1, f1, "xk")
                stage(x1_factors, 2)

            run(pool, body)


_INS = ['L0_attn_x', 'L0_attn_Wq', 'L0_attn_bq', 'L0_attn_Wk', 'L0_attn_bk', 'L0_attn_Wv', 'L0_attn_bv',
        'L0_attn_Wc', 'L0_attn_We', 'L0_attn_Wo', 'L0_attn_bo', 'L0_attn_gamma', 'L0_attn_beta',
        'L0_ffn_W_r', 'L0_ffn_W_k', 'L0_ffn_W_v', 'L0_ffn_mu_r', 'L0_ffn_mu_k']


def kernel(**inputs):
    import numpy as _np
    import concourse.bacc as _bacc
    from concourse import mybir as _mybir
    from concourse.bass_utils import run_bass_kernel_spmd as _run

    nc = _bacc.Bacc("TRN2", target_bir_lowering=False, num_devices=1)
    arrays, args = {}, []
    for name in _INS:
        a = _np.ascontiguousarray(inputs[name])
        arrays[f"in_{name}_dram"] = a
        args.append(nc.dram_tensor(f"in_{name}_dram", a.shape, _mybir.dt.from_np(a.dtype), kind="ExternalInput").ap())
    shape = inputs['L0_attn_x'].shape
    args.append(nc.dram_tensor("out_0_dram", shape, _mybir.dt.float32, kind="ExternalOutput").ap())
    macaron_program(nc, *args)
    r = _run(nc, [arrays], core_ids=[0])
    return r.results[0]["out_0_dram"]
```

```python
from contextlib import ExitStack

import concourse.bass as bass
from concourse import mybir

F32 = mybir.dt.float32
F32R = mybir.dt.float32r
ALU = mybir.AluOpType
ACT = mybir.ActivationFunctionType

P = 128
EPS_LN = 1e-5
EPS_DEN = 1e-6


def macaron_program(nc, x, Wq, bq, Wk, bk, Wv, bv, Wc, We, Wo, bo, gamma, beta, W_r, W_k, W_v, mu_r, mu_k, out):
    B, S, D = x.shape
    KV = Wk.shape[1]
    HD = 16
    J = KV // HD
    G = D // KV
    C = 32
    NC = P // C
    V1 = HD + 1
    VW = J * V1
    CI = D // P
    NB = B // 2
    NT = S // P
    STEPS = NB * NT
    assert D == CI * P and J * C == P and 2 * KV == P and STEPS % 2 == 0

    ctx = ExitStack()
    with ctx:
        def sb(name, *shape):
            return ctx.enter_context(nc.sbuf_tensor(name, list(shape), F32))

        def sbr(name, *shape):
            return ctx.enter_context(nc.sbuf_tensor(name, list(shape), F32R))

        def sem(name):
            return ctx.enter_context(nc.semaphore(name))

        wr_raw, wk_raw, wv_raw = (sb(f"{n}_raw", P, CI, D) for n in ("wr", "wk", "wv"))
        wrT, wkT, wvT = (sbr(f"{n}T", P, 2, CI, D) for n in ("wr", "wk", "wv"))
        w_full = sb("w_full", P, 3, CI, D)
        wo_s = sbr("wo_s", P, 2, CI, D)
        wq_raw = sb("wq_raw", P, CI, D)
        wo_p = sb("wo_p", P, CI, D)
        kraw, vraw = sb("kraw", P, CI, KV), sb("vraw", P, CI, KV)
        kvrawT = sb("kvrawT", KV, 2, CI, P)
        wc_sb, we_sb, wcT, wce = (sb(n, KV, KV) for n in ("wc_sb", "we_sb", "wcT", "wce"))
        wkvq = sb("wkvq", P, CI, 2 * KV + D)
        wkvq_s = sbr("wkvq_s", P, 2, CI, 2 * KV + D)
        bkc, bvc = sb("bkc", KV, 1), sb("bvc", KV, 1)
        bk1_rep, bv_rep = sb("bk1_rep", P, KV), sb("bv_rep", P, KV)
        bq_rep, bq1_rep = sb("bq_rep", P, D), sb("bq1_rep", P, G, KV)
        bo_rep, gamma_rep, beta_rep = sb("bo_rep", P, D), sb("gamma_rep", P, D), sb("beta_rep", P, D)
        mur, muk = sb("mur", P, CI), sb("muk", P, CI)
        ident = sb("ident", P, P)
        causal = sb("causal", P, C)
        vmask = sb("vmask", P, J, HD)
        smask = sb("smask", P, J, V1)
        kmask = sb("kmask", P, J)
        spread = sb("spread", P, NC, J, C)
        eps_ln, spacer = sb("eps_ln", P, 2), sb("spacer", P, 1)
        neg_one = sb("neg_one", P, 2)
        neg_half = sb("neg_half", P, 2)

        class Ffn:
            pass

        def ffn_buffers(n):
            f = Ffn()
            f.stats, f.mv = sb(f"{n}_stats", P, 2, 6), sb(f"{n}_mv", P, 2, 2)
            f.veps, f.rstd = sb(f"{n}_veps", P, 2), sb(f"{n}_rstd", P, 2)
            f.negm, f.nmr = sb(f"{n}_negm", P, 2), sb(f"{n}_nmr", P, 2)
            f.h = sb(f"{n}_h", P, 2, D)
            f.hT = sb(f"{n}_hT", P, CI, 2, P + 1)
            f.carry = sb(f"{n}_carry", P, NT + 1, CI, 2)
            f.d = sb(f"{n}_d", P, CI, 2, P)
            f.xk, f.xr = sb(f"{n}_xk", P, CI, 2, P), sb(f"{n}_xr", P, CI, 2, P)
            f.relu, f.ka = sb(f"{n}_relu", P, CI, 2, P), sb(f"{n}_ka", P, CI, 2, P)
            f.xk_s, f.xr_s, f.ka_s = (sbr(f"{n}_{v}_s", P, 2, CI, 2, P) for v in ("xk", "xr", "ka"))
            f.full = {"xk": f.xk, "xr": f.xr, "ka": f.ka}
            f.split = {"xk": f.xk_s, "xr": f.xr_s, "ka": f.ka_s}
            f.th, f.t1 = sb(f"{n}_th", P, 2, D), sb(f"{n}_t1", P, 2, D)
            f.s = {s: sem(f"{n}_{s}_done") for s in
                   ("stats", "mv", "veps", "rstd", "nmr", "h", "hTp", "hT", "edge", "d", "xk", "xr",
                    "xk_hi", "xk_lo", "xr_hi", "xr_lo", "kp", "relu", "ka", "ka_hi", "ka_lo", "rp", "th", "vp",
                    "t1", "y")}
            return f

        f1, f2 = ffn_buffers("f1"), ffn_buffers("f2")
        x_in = sb("x_in", P, NT, 2, D)
        x1 = sb("x1", P, 2, 2, D)
        x2 = sb("x2", P, 2, 2, D)
        x3 = sb("x3", P, 2, 2, D)

        a_stats, a_mv = sb("a_stats", P, 2, 6), sb("a_mv", P, 2, 2)
        a_veps, a_rstd, a_negm, a_nmr = (sb(f"a_{n}", P, 2) for n in ("veps", "rstd", "negm", "nmr"))
        h2 = sb("h2", P, 2, D)
        h2b = sb("h2b", P, 2, 2, D)
        x1b = sb("x1b", P, 2, 2, D)
        h2T_s = sbr("h2T_s", P, 2, CI, 2, P)
        yk, ek = sb("yk", P, 2, KV), sb("ek", P, 2, KV)
        kf = sb("kf", P, 2, KV)
        vaug = sb("vaug", P, 2, 2, J, V1)
        kbd = sb("kbd", P, NC, J, C)
        yq, eq, qt = (sb(n, P, G, 2, KV) for n in ("yq", "eq", "qt"))
        qf = sb("qf", P, 2, NC, G, C)
        vbd = sb("vbd", P, 2, NC, J, V1)
        am = sb("am", P, 2, NC, G, C)
        sp = sb("sp", P, NC, VW)
        st = sb("st", P, 2, NC, VW)
        st_carry = sb("st_carry", P, NT + 1, VW)
        den, rden = sb("den", P, 2, J * G), sb("rden", P, 2, J * G)
        attn = sb("attn", P, 2, D)
        attnT_s = sbr("attnT_s", P, 2, CI, 2, P)
        y = sb("y", P, 2, D)
        y_stats, y_mv = sb("y_stats", P, 2, 6), sb("y_mv", P, 2, 2)
        y_veps, y_rstd = sb("y_veps", P, 2), sb("y_rstd", P, 2)
        z = sb("z", P, 2, D)

        def psum(name):
            return ctx.enter_context(nc.psum_tensor(name, [P, 512], F32))

        bank_T, bank_K, bank_R, bank_V, bank_Q, bank_KV, bank_0, bank_1 = (
            psum(n) for n in ("bank_T", "bank_K", "bank_R", "bank_V", "bank_Q", "bank_KV", "bank_0", "bank_1"))
        psT = bank_T[:, :].rearrange("q (c p t) -> q c p t", c=CI, p=2)
        psK = bank_K[:, :].rearrange("q (c n) -> q c n", c=CI)
        psR = bank_R[:, :].rearrange("q (p d) -> q p d", p=2)
        psV = bank_V[:, :].rearrange("q (p d) -> q p d", p=2)
        psQ = bank_Q[:, :].rearrange("q (g t) -> q g t", g=G)
        psKVQ = [b[:, 0:2 * KV + D] for b in (bank_KV, bank_Q)]
        psKT = bank_KV[:, 0:P]
        psS = bank_KV[:, 0:NC * VW].rearrange("q (c n) -> q c n", c=NC)
        psO = [b[:, 0:G * VW].rearrange("q (g j d) -> q g j d", g=G, j=J) for b in (bank_Q, bank_KV)]
        psVB = bank_0[:, :].rearrange("q (c p n) -> q c p n", c=NC, p=2)
        psA = [b[:, :].rearrange("q (c g t) -> q c g t", c=NC, g=G) for b in (bank_0, bank_1)]
        psOT = bank_1[:, :].rearrange("q (c p t) -> q c p t", c=CI, p=2)
        psW = bank_1[:, :].rearrange("q (p d) -> q p d", p=2)

        ffn_loaded, w_loaded = sem("ffn_loaded"), sem("w_loaded")
        x_loaded, stored = [sem("x_loaded0"), sem("x_loaded1")], [sem("stored0"), sem("stored1")]
        consts = sem("consts")
        mask_step = sem("mask_step")
        wT_done, w_full_done, w_hi_done, wk_lo_done, wrv_lo_done = (
            sem(n) for n in ("wT_done", "w_full_done", "w_hi_done", "wk_lo_done", "wrv_lo_done"))
        wo_split = sem("wo_split")
        setup_pe, setup_dve = sem("setup_pe"), sem("setup_dve")
        A = {n: sem(f"a_{n}_done") for n in (
            "stats", "mv", "veps", "rstd", "nmr", "h", "hTp", "hT", "hT_lo", "h2b", "x1b", "kvqp", "qT", "qTp", "yk", "vaug",
            "ek", "kf", "kTp", "kbd", "yq", "eq", "qf", "vbp", "vb", "Sp", "sp",
            "st0", "st", "stc", "A0p", "A1p", "A0", "A1", "O0p", "O1p", "den0", "den1", "rden0", "rden1",
            "o0", "o1", "oTp", "oT_hi", "oT_lo", "wp", "y", "ystats", "ymv", "yveps", "yrstd", "z", "x2")}

        x_dram = x.rearrange("(p b) (n t) c -> b n t p c", p=2, t=P)
        out_dram = out.rearrange("(p b) (n t) c -> b n t p c", p=2, t=P)
        ffn_loads, loads = [], []

        def row(v):
            return v.rearrange("(a c) -> a c", a=1)

        for dst, src in ((wk_raw, W_k), (wr_raw, W_r), (wv_raw, W_v)):
            ffn_loads.append((dst[:], src.rearrange("(o q) c -> q o c", q=P)))
        for dst, src in ((muk, mu_k), (mur, mu_r)):
            ffn_loads.append((dst[:], src.rearrange("(c q) -> q c", q=P)))
        for dst, src in ((kraw, Wk), (vraw, Wv)):
            loads.append((dst[:], src.rearrange("(o q) c -> q o c", q=P)))
        for dst, src in ((wc_sb, Wc), (we_sb, We)):
            loads.append((dst[:], src))
        for dst, src in ((bkc, bk), (bvc, bv)):
            loads.append((dst[:], src.rearrange("(q a) -> q a", a=1)))
        loads.append((wq_raw[:], Wq.rearrange("(o q) c -> q o c", q=P)))
        for dst, src in ((bq_rep, bq), (bo_rep, bo), (beta_rep, beta), (gamma_rep, gamma)):
            loads.append((dst[:], row(src).broadcast_to([P, D])))
        for gp in range(2):
            for j in range(J):
                q0 = gp * KV + j * HD
                loads.append((wo_p[q0:q0 + HD],
                              Wo.rearrange("(j gc gp d) c -> j gp d gc c", j=J, gc=CI, gp=2)[j, gp]))
        FFN_ALL, W_ALL = 16 * len(ffn_loads), 16 * len(loads)

        LAST = STEPS - 1
        MAX_LAG = 5
        DVE_SETUP_STEPS = 8

        def run(eng, body, setups={}, max_lag=MAX_LAG):
            first = max_lag + 2 - max_lag % 2

            def iteration(i, u):
                def stage(work, lag, *args):
                    if has(i - lag):
                        work(i - lag, (u - lag) % 2, *args)
                body(stage)

            for i in range(first):
                if i in setups:
                    setups[i]()
                iteration(i, i % 2)
            with eng.Fori(first // 2, STEPS // 2) as m:
                for u in range(2):
                    iteration(m * 2 + u, u)
            for i in range(STEPS, STEPS + max_lag + 1):
                iteration(i, i % 2)

        def has(k):
            return not isinstance(k, int) or 0 <= k <= LAST

        def upto(k):
            return min(k, LAST) + 1 if isinstance(k, int) else k + 1

        block = ctx.enter_context(nc.Block())

        @block.sync
        def _(sp_eng):
            def load(k, q):
                sp_eng.dma_start(x_in[:, k % NT], x_dram[k // NT, k % NT]).then_inc(x_loaded[q], 16)

            load(0, 0)
            for dst, src in ffn_loads:
                sp_eng.dma_start(dst, src, allow_slow_non_contiguous=True).then_inc(ffn_loaded, 16)
            load(1, 1)
            for dst, src in loads:
                sp_eng.dma_start(dst, src, allow_slow_non_contiguous=True).then_inc(w_loaded, 16)

            def load_next(k, q):
                if has(k - 2):
                    sp_eng.wait_ge(f1.s["stats"], upto(k - 2))
                    load(k, q)

            def store(k, q):
                sp_eng.wait_ge(f2.s["y"], upto(k))
                sp_eng.dma_start(out_dram[k // NT, k % NT], x3[:, q]).then_inc(stored[q], 16)

            def body(stage):
                stage(load_next, 0)
                stage(store, 7)

            run(sp_eng, body, max_lag=7)
            for u in range(2):
                sp_eng.wait_ge(stored[u], 16 * (STEPS // 2))

        @block.tensor
        def _(pe):
            mm, tr = nc.tensor.matmul, nc.tensor.transpose

            pe.wait_ge(consts, 1)
            pe.wait_ge(ffn_loaded, FFN_ALL)
            for raw, bank in ((wk_raw, bank_K), (wr_raw, bank_R), (wv_raw, bank_V)):
                for ci in range(CI):
                    for do in range(CI):
                        last = tr(bank[:, ci * D + do * P:ci * D + (do + 1) * P],
                                  raw[:, do, ci * P:(ci + 1) * P], ident[:])
                last.then_inc(wT_done, 1)

            def attention_weights():
                pe.wait_ge(w_loaded, W_ALL)
                for n, raw in enumerate((kraw, vraw)):
                    for ci in range(CI):
                        last = tr(bank_Q[0:KV, (n * CI + ci) * P:(n * CI + ci + 1) * P], raw[:, ci, :], ident[:])
                last.then_inc(setup_pe, 1)
                tr(bank_KV[0:KV, 0:KV], wc_sb[:], ident[0:KV, 0:KV]).then_inc(setup_pe, 1)
                pe.wait_ge(setup_dve, 2)
                mm(bank_0[0:KV, 0:KV], wcT[:], we_sb[:], start=True, stop=True).then_inc(setup_pe, 1)
                pe.wait_ge(setup_dve, 3)
                for ci in range(CI):
                    for n in range(2):
                        o = ci * 2 * KV + n * KV
                        last = mm(bank_1[:, o:o + KV], kvrawT[:, n, ci, :], wce[:], start=True, stop=True)
                last.then_inc(setup_pe, 1)
                for n, b in enumerate((bkc, bvc)):
                    last = mm(bank_KV[:, n * KV:(n + 1) * KV], b[:].broadcast_to([KV, P]), wce[:],
                              start=True, stop=True)
                last.then_inc(setup_pe, 1)

            def weights_split(n):
                pe.wait_ge(w_hi_done, n + 1)
                if n == 0:
                    pe.wait_ge(wk_lo_done, 1)
                else:
                    pe.wait_ge(wrv_lo_done, n)

            def products(out_of, lhs_of, rhs_of):
                terms = [(hl, hr, ci) for hl, hr in ((0, 0), (0, 1), (1, 0)) for ci in range(CI)]
                for n, (hl, hr, ci) in enumerate(terms):
                    last = mm(out_of, lhs_of(hl, ci), rhs_of(hr, ci), start=n == 0, stop=n == len(terms) - 1)
                return last

            def bank_free(evacuated, k):
                if has(k):
                    pe.wait_ge(evacuated, upto(k))

            def transposes(ps, src, done):
                for p in range(2):
                    for ci in range(CI):
                        last = tr(ps[:, ci, p, :], src[:, p, ci * P:(ci + 1) * P], ident[:])
                last.then_inc(done, 1)

            def ffn_T1(k, q):
                pe.wait_ge(f1.s["h"], upto(k))
                bank_free(A["hT_lo"], k - 2)
                transposes(psT, f1.h, f1.s["hTp"])

            def ffn_T2(k, q):
                pe.wait_ge(f2.s["h"], upto(k))
                bank_free(f1.s["hT"], k + 3)
                transposes(psT, f2.h, f2.s["hTp"])

            def ffn_K(k, q, f, other, other_k):
                pe.wait_ge(f.s["xk_hi"], upto(k))
                pe.wait_ge(f.s["xk_lo"], upto(k))
                bank_free(other.s["relu"], k + other_k)
                if f is f1 and isinstance(k, int) and k == 0:
                    weights_split(0)
                for co in range(CI):
                    last = products(psK[:, co, :], lambda h, ci: wkT[:, h, ci, co * P:(co + 1) * P],
                                    lambda h, ci: f.xk_s[:, h, ci].rearrange("q p t -> q (p t)"))
                last.then_inc(f.s["kp"], 1)

            def ffn_R(k, q, f, other, other_k):
                pe.wait_ge(f.s["xr_hi"], upto(k))
                pe.wait_ge(f.s["xr_lo"], upto(k))
                bank_free(other.s["th"], k + other_k)
                if f is f1 and isinstance(k, int) and k == 0:
                    weights_split(1)
                for p in range(2):
                    last = products(psR[:, p, :], lambda h, ci: f.xr_s[:, h, ci, p, :], lambda h, ci: wrT[:, h, ci, :])
                last.then_inc(f.s["rp"], 1)

            def ffn_V(k, q, f, other, other_k):
                pe.wait_ge(f.s["ka_hi"], upto(k))
                pe.wait_ge(f.s["ka_lo"], upto(k))
                bank_free(other.s["t1"], k + other_k)
                if f is f1 and isinstance(k, int) and k == 0:
                    weights_split(2)
                for p in range(2):
                    last = products(psV[:, p, :], lambda h, ci: f.ka_s[:, h, ci, p, :], lambda h, ci: wvT[:, h, ci, :])
                last.then_inc(f.s["vp"], 1)

            def attn_T(k, q):
                pe.wait_ge(A["h"], upto(k))
                bank_free(f2.s["hT"], k - 2)
                transposes(psT, h2, A["hTp"])

            def kvq_product(k, q):
                pe.wait_ge(A["hT"], upto(k))
                pe.wait_ge(A["hT_lo"], upto(k))
                if isinstance(k, int) and k == 0:
                    pe.wait_ge(setup_dve, DVE_SETUP_STEPS)
                bank_free(A["o0"], k - 1)
                bank_free(A["o1"], k - 1)
                for p in range(2):
                    last = products(psKVQ[p], lambda h, ci: h2T_s[:, h, ci, p, :], lambda h, ci: wkvq_s[:, h, ci, :])
                last.then_inc(A["kvqp"], 1)

            def q_transpose(k, q):
                pe.wait_ge(A["qT"], upto(k))
                for g in range(G):
                    last = tr(psQ[:, g, :], qt[:, g].rearrange("q p n -> q (p n)"), ident[:])
                last.then_inc(A["qTp"], 1)

            def k_transpose(k, q):
                pe.wait_ge(A["kf"], upto(k))
                pe.wait_ge(A["vaug"], upto(k))
                pe.wait_ge(A["yq"], upto(k))
                tr(psKT, kf[:].rearrange("q p n -> q (p n)"), ident[:]).then_inc(A["kTp"], 1)

            def v_spread(k, q):
                pe.wait_ge(A["vaug"], upto(k))
                bank_free(A["A0"], k - 1)
                for n in range(NC):
                    last = mm(psVB[:, n].rearrange("q p (j d) -> q p j d", j=J),
                              spread[:, n].rearrange("q j s -> q (j s)"),
                              vaug[:, q, :, :, 0:HD], start=True, stop=True)
                last.then_inc(A["vbp"], 1)

            def state_growth(k, q):
                pe.wait_ge(A["kbd"], upto(k))
                for n in range(NC):
                    for p in range(2):
                        last = mm(psS[p * KV:(p + 1) * KV, n, :], kf[0:(n + 1) * C, p, :],
                                  vaug[0:(n + 1) * C, q, p].rearrange("q j d -> q (j d)"),
                                  start=True, stop=True)
                last.then_inc(A["Sp"], 1)

            def scores(k, q, p):
                pe.wait_ge(A["qf"], upto(k))
                pe.wait_ge(A["kbd"], upto(k))
                if p == 0:
                    pe.wait_ge(A["vb"], upto(k))
                else:
                    bank_free(A["y"], k - 1)
                for n in range(NC):
                    last = mm(psA[p][:, n].rearrange("q g t -> q (g t)"),
                              kbd[p * KV:(p + 1) * KV, n].rearrange("q j s -> q (j s)"),
                              qf[p * KV:(p + 1) * KV, q, n].rearrange("q g t -> q (g t)"), start=True, stop=True)
                last.then_inc(A[f"A{p}p"], 1)

            def attend(k, q, p):
                pe.wait_ge(A[f"A{p}"], upto(k))
                pe.wait_ge(A["vb"], upto(k))
                pe.wait_ge(A["st"], upto(k))
                for g in range(G):
                    for n in range(NC):
                        mm(psO[p][n * C:(n + 1) * C, g].rearrange("q j d -> q (j d)"), am[:, p, n, g, :],
                           vbd[:, p, n].rearrange("q j d -> q (j d)"), start=g == 0, stop=False,
                           skip_group_check=True, tile_position=(0, n * C))
                for g in range(G):
                    for n in range(NC):
                        last = mm(psO[p][n * C:(n + 1) * C, g].rearrange("q j d -> q (j d)"),
                                  qf[p * KV:(p + 1) * KV, q, n, g, :], st[p * KV:(p + 1) * KV, q, n, :],
                                  start=False, stop=g == G - 1, skip_group_check=True,
                                  tile_position=(p * KV, n * C))
                last.then_inc(A[f"O{p}p"], 1)

            def output_transpose(k, q):
                for p in range(2):
                    pe.wait_ge(A[f"o{p}"], upto(k))
                pe.wait_ge(A["A1"], upto(k))
                transposes(psOT, attn, A["oTp"])

            def output_product(k, q):
                pe.wait_ge(A["oT_hi"], upto(k))
                pe.wait_ge(A["oT_lo"], upto(k))
                if isinstance(k, int) and k == 0:
                    pe.wait_ge(wo_split, 2)
                for p in range(2):
                    last = products(psW[:, p, :], lambda h, ci: attnT_s[:, h, ci, p, :], lambda h, ci: wo_s[:, h, ci, :])
                last.then_inc(A["wp"], 1)

            def body(stage):
                stage(scores, 3, 0)
                stage(attend, 3, 1)
                stage(attend, 3, 0)
                stage(ffn_K, 4, f2, f1, 2)
                stage(output_transpose, 3)
                stage(attn_T, 2)
                stage(ffn_K, 1, f1, f2, -3)
                stage(output_product, 3)
                stage(kvq_product, 2)
                stage(ffn_R, 4, f2, f1, 2)
                stage(ffn_T1, 0)
                stage(v_spread, 2)
                stage(ffn_V, 4, f2, f1, 2)
                stage(k_transpose, 2)
                stage(ffn_R, 1, f1, f2, -3)
                stage(state_growth, 2)
                stage(q_transpose, 2)
                stage(ffn_T2, 3)
                stage(ffn_V, 1, f1, f2, -3)
                stage(scores, 2, 1)

            run(pe, body, {2: attention_weights})

        @block.scalar
        def _(act):
            activation = nc.scalar.activation

            def normalise(s, k, dst, src, rstd, nmr):
                act.wait_ge(s["nmr"], upto(k))
                for p in range(2):
                    last = activation(dst[:, p, :], src[:, p, :], ACT.Identity, bias=nmr[:, p:p + 1],
                                      scale=rstd[:, p:p + 1])
                last.then_inc(s["h"], 1)

            def normalise_x(k, q):
                normalise(f1.s, k, f1.h, x_in[:, k % NT], f1.rstd, f1.nmr)

            def normalise_x1(k, q):
                normalise(A, k, h2, x1[:, q], a_rstd, a_nmr)

            def normalise_x2(k, q):
                normalise(f2.s, k, f2.h, x2[:, q], f2.rstd, f2.nmr)

            def evacuate_hT(k, q, f):
                act.wait_ge(f.s["hTp"], upto(k))
                activation(f.hT[:, :, :, 1:], psT, ACT.Copy).then_inc(f.s["hT"], 1)

            def evacuate_h2T(k, q):
                act.wait_ge(A["hTp"], upto(k))
                activation(h2T_s[:, 0], psT, ACT.Copy).then_inc(A["hT"], 1)

            def high(k, q, f, name):
                act.wait_ge(f.s[name], upto(k))
                activation(f.split[name][:, 0], f.full[name][:], ACT.Copy).then_inc(f.s[f"{name}_hi"], 1)

            def k_relu(k, q, f):
                act.wait_ge(f.s["kp"], upto(k))
                activation(f.relu[:].rearrange("q c p t -> q (c p t)"), bank_K[:, :], ACT.Relu).then_inc(f.s["relu"], 1)

            def k_square(k, q, f):
                act.wait_ge(f.s["relu"], upto(k))
                activation(f.ka[:], f.relu[:], ACT.Square).then_inc(f.s["ka"], 1)

            def r_tanh(k, q, f):
                act.wait_ge(f.s["rp"], upto(k))
                activation(f.th[:], psR, ACT.Tanh, scale=0.5).then_inc(f.s["th"], 1)

            def exp_k(k, q):
                act.wait_ge(A["yk"], upto(k))
                activation(ek[:], yk[:], ACT.Exp, bias=-1.0).then_inc(A["ek"], 1)

            def evacuate_q(k, q):
                act.wait_ge(A["qTp"], upto(k))
                activation(qf[:, q].rearrange("q c g t -> q g c t"), psQ.rearrange("q g (c t) -> q g c t", c=NC),
                           ACT.Copy).then_inc(A["qf"], 1)

            def exp_q(k, q):
                act.wait_ge(A["yq"], upto(k))
                activation(eq[:], yq[:], ACT.Exp, bias=-1.0).then_inc(A["eq"], 1)

            def block_diagonal_k(k, q):
                act.wait_ge(A["kTp"], upto(k))
                for j in range(J):
                    last = activation(kbd[:, :, j, :], psKT.rearrange("q (c s) -> q c s", c=NC), ACT.Identity,
                                      scale=kmask[:, j:j + 1])
                last.then_inc(A["kbd"], 1)

            def output_high(k, q):
                act.wait_ge(A["oTp"], upto(k))
                activation(attnT_s[:, 0], psOT, ACT.Copy).then_inc(A["oT_hi"], 1)

            def body(stage):
                stage(k_relu, 2, f1)
                stage(k_square, 2, f1)
                stage(high, 2, f1, "ka")
                stage(exp_k, 3)
                stage(evacuate_hT, 1, f1)
                stage(r_tanh, 5, f2)
                stage(exp_q, 3)
                stage(block_diagonal_k, 3)
                stage(normalise_x2, 4)
                stage(evacuate_q, 3)
                stage(evacuate_hT, 4, f2)
                stage(r_tanh, 2, f1)
                stage(high, 4, f2, "xk")
                stage(high, 1, f1, "xk")
                stage(normalise_x1, 2)
                stage(k_relu, 4, f2)
                stage(output_high, 3)
                stage(evacuate_h2T, 2)
                stage(high, 4, f2, "xr")
                stage(high, 1, f1, "xr")
                stage(normalise_x, 0)
                stage(k_square, 4, f2)
                stage(high, 4, f2, "ka")

            def ffn_weights():
                for n, split in enumerate((wkT, wrT, wvT)):
                    act.wait_ge(w_full_done, n + 1)
                    activation(split[:, 0], w_full[:, n], ACT.Copy).then_inc(w_hi_done, 1)

            def masks_there():
                act.wait_ge(consts, 3)

            run(act, body, {1: ffn_weights, 3: masks_there})

        @block.vector
        def _(dve):
            v = nc.vector

            def ffn_weights():
                for n, (bank, factor) in enumerate(((bank_K, 1.0), (bank_R, 1.0), (bank_V, 0.25))):
                    dve.wait_ge(wT_done, n + 1)
                    v.tensor_scalar(w_full[:, n].rearrange("q c d -> q (c d)"), bank[:, :], factor, None,
                                    ALU.mult).then_inc(w_full_done, 1)
                dve.wait_ge(consts, 2)

            def ffn_low_parts():
                for n, split in ((1, wrT), (2, wvT)):
                    dve.wait_ge(w_hi_done, n + 1)
                    v.tensor_tensor(split[:, 1], w_full[:, n], split[:, 0].bitcast(F32),
                                    ALU.subtract).then_inc(wrv_lo_done, 1)

            def attention_weights():
                dve.wait_ge(setup_pe, 1)
                v.tensor_copy(kvrawT[:].rearrange("q n c d -> q (n c d)"), bank_Q[0:KV, :]).then_inc(setup_dve, 1)
                dve.wait_ge(setup_pe, 2)
                v.tensor_copy(wcT[:], bank_KV[0:KV, 0:KV]).then_inc(setup_dve, 1)
                dve.wait_ge(setup_pe, 3)
                v.tensor_copy(wce[:], bank_0[0:KV, 0:KV]).then_inc(setup_dve, 1)
                dve.wait_ge(w_loaded, W_ALL)
                dve.wait_ge(consts, 3)
                for ci in range(CI):
                    v.tensor_copy(wkvq[:, ci, 2 * KV:].rearrange("q (g j f) -> q g j f", g=G, j=J),
                                  wq_raw[:, ci].rearrange("q (j g f) -> q g j f", j=J, g=G))
                v.tensor_scalar(bq1_rep[:].rearrange("q g (j f) -> q g j f", j=J),
                                bq_rep[:].rearrange("q (j g f) -> q g j f", j=J, g=G), 1.0, None, ALU.add)
                v.tensor_copy(spread[:], ident[:].rearrange("q (c s) -> q c s", c=NC).unsqueeze(2)
                              .broadcast_to([P, NC, J, C]))
                v.tensor_copy(vbd[:, :, :, :, HD].rearrange("q p c j -> q (p c) j"),
                              vmask[:, :, 0].unsqueeze(1).broadcast_to([P, 2 * NC, J])).then_inc(setup_dve, 1)
                dve.wait_ge(setup_pe, 4)
                v.tensor_copy(wkvq[:, :, 0:2 * KV], bank_1[:, 0:CI * 2 * KV].rearrange("q (c d) -> q c d", c=CI)
                              ).then_inc(setup_dve, 1)
                dve.wait_ge(setup_pe, 5)
                v.tensor_scalar(bk1_rep[:], bank_KV[:, 0:KV], 1.0, None, ALU.add)
                v.tensor_copy(bv_rep[:], bank_KV[:, KV:2 * KV]).then_inc(setup_dve, 1)
                dve.wait_ge(setup_dve, 5)
                v.tensor_copy(wkvq_s[:, 0], wkvq[:]).then_inc(setup_dve, 1)
                dve.wait_ge(setup_dve, 7)
                v.tensor_tensor(wkvq_s[:, 1], wkvq[:], wkvq_s[:, 0].bitcast(F32), ALU.subtract).then_inc(setup_dve, 1)
                dve.wait_ge(setup_dve, DVE_SETUP_STEPS)

            def output_weights():
                v.tensor_copy(wo_s[:, 0], wo_p[:]).then_inc(wo_split, 1)
                dve.wait_ge(wo_split, 1)
                v.tensor_tensor(wo_s[:, 1], wo_p[:], wo_s[:, 0].bitcast(F32), ALU.subtract).then_inc(wo_split, 1)

            def statistics(src, stats, mv, s, stats_name, mv_name, k):
                for p in range(2):
                    last = v.bn_stats(stats[:, p, :], src[:, p, :])
                last.then_inc(s[stats_name], 1)
                dve.wait_ge(s[stats_name], upto(k))
                v.memset(spacer[:], 0.0)
                for p in range(2):
                    last = v.bn_aggr(mv[:, p, :], stats[:, p, :])
                last.then_inc(s[mv_name], 1)

            def x_statistics(k, q):
                if has(k - 1):
                    dve.wait_ge(f1.s["nmr"], upto(k - 1))
                dve.wait_ge(x_loaded[q], 16 * (k // 2 + 1))
                statistics(x_in[:, k % NT], f1.stats, f1.mv, f1.s, "stats", "mv", k)

            def x1_statistics(k, q):
                dve.wait_ge(f1.s["y"], upto(k))
                statistics(x1[:, q], a_stats, a_mv, A, "stats", "mv", k)

            def x2_statistics(k, q):
                dve.wait_ge(A["x2"], upto(k))
                statistics(x2[:, q], f2.stats, f2.mv, f2.s, "stats", "mv", k)

            def difference(k, q, f):
                n = k % NT
                dve.wait_ge(f.s["hT"], upto(k))
                v.tensor_copy(f.hT[:, :, :, 0], f.carry[:, n]).then_inc(f.s["edge"], 1)
                v.tensor_copy(f.carry[:, n + 1], f.hT[:, :, :, P])
                dve.wait_ge(f.s["edge"], upto(k))
                v.tensor_tensor(f.d[:], f.hT[:, :, :, 1:], f.hT[:, :, :, 0:P], ALU.subtract).then_inc(f.s["d"], 1)

            def mix(k, q, f, name, mu):
                dve.wait_ge(f.s["d"], upto(k))
                for ci in range(CI):
                    last = v.scalar_tensor_tensor(out=f.full[name][:, ci], in0=f.d[:, ci], scalar=mu[:, ci:ci + 1],
                                                  in1=f.hT[:, ci, :, 0:P], op0=ALU.mult, op1=ALU.add)
                last.then_inc(f.s[name], 1)

            def low(k, q, f, name):
                dve.wait_ge(f.s[f"{name}_hi"], upto(k))
                v.tensor_tensor(f.split[name][:, 1], f.full[name][:], f.split[name][:, 0].bitcast(F32),
                                ALU.subtract).then_inc(f.s[f"{name}_lo"], 1)

            def gate(k, q, f):
                dve.wait_ge(f.s["th"], upto(k))
                dve.wait_ge(f.s["vp"], upto(k))
                v.scalar_tensor_tensor(out=f.t1[:], in0=f.th[:], scalar=1.0, in1=psV, op0=ALU.add,
                                       op1=ALU.mult).then_inc(f.s["t1"], 1)

            def k_bias(k, q):
                dve.wait_ge(A["kvqp"], upto(k))
                for p in range(2):
                    last = v.tensor_tensor(yk[:, p], psKVQ[p][:, 0:KV], bk1_rep[:], ALU.add)
                last.then_inc(A["yk"], 1)

            def v_bias(k, q):
                dve.wait_ge(A["kvqp"], upto(k))
                for p in range(2):
                    last = v.tensor_tensor(vaug[:, q, p, :, 0:HD],
                                           psKVQ[p][:, KV:2 * KV].rearrange("q (j d) -> q j d", j=J),
                                           bv_rep[:].rearrange("q (j d) -> q j d", j=J), ALU.add)
                last.then_inc(A["vaug"], 1)

            def q_bias(k, q):
                dve.wait_ge(A["kvqp"], upto(k))
                for p in range(2):
                    last = v.tensor_tensor(yq[:, :, p, :], psKVQ[p][:, 2 * KV:].rearrange("q (g n) -> q g n", g=G),
                                           bq1_rep[:], ALU.add)
                last.then_inc(A["yq"], 1)

            def h2_low(k, q):
                dve.wait_ge(A["hT"], upto(k))
                v.tensor_tensor(h2T_s[:, 1], psT, h2T_s[:, 0].bitcast(F32), ALU.subtract).then_inc(A["hT_lo"], 1)

            def k_feature(k, q):
                dve.wait_ge(A["ek"], upto(k))
                v.scalar_tensor_tensor(out=kf[:], in0=yk[:], scalar=1.0, in1=ek[:], op0=ALU.max,
                                       op1=ALU.min).then_inc(A["kf"], 1)

            def q_feature(k, q):
                dve.wait_ge(A["eq"], upto(k))
                v.scalar_tensor_tensor(out=qt[:], in0=yq[:], scalar=1.0, in1=eq[:], op0=ALU.max,
                                       op1=ALU.min).then_inc(A["qT"], 1)

            def block_diagonal_v(k, q):
                dve.wait_ge(A["vbp"], upto(k))
                for p in range(2):
                    last = v.tensor_tensor(vbd[:, p, :, :, 0:HD], psVB[:, :, p].rearrange("q c (j d) -> q c j d", j=J),
                                           vmask[:].unsqueeze(1).broadcast_to([P, NC, J, HD]), ALU.mult)
                last.then_inc(A["vb"], 1)

            def mask_state(k, q):
                dve.wait_ge(A["Sp"], upto(k))
                v.tensor_tensor(sp[:], psS,
                                smask[:].rearrange("q j d -> q (j d)").unsqueeze(1).broadcast_to([P, NC, VW]),
                                ALU.mult).then_inc(A["sp"], 1)

            def causal_mask(k, q, p):
                dve.wait_ge(A[f"A{p}p"], upto(k))
                v.tensor_tensor(am[:, p].rearrange("q c g t -> q (c g) t"), psA[p].rearrange("q c g t -> q (c g) t"),
                                causal[:].unsqueeze(1).broadcast_to([P, NC * G, C]), ALU.mult).then_inc(A[f"A{p}"], 1)

            def normalise_output(k, q, p):
                dve.wait_ge(A[f"O{p}p"], upto(k))
                v.tensor_scalar(den[:, p].rearrange("q (g j) -> q g j", g=G), psO[p][:, :, :, HD], EPS_DEN, None,
                                ALU.add).then_inc(A[f"den{p}"], 1)
                dve.wait_ge(A[f"den{p}"], upto(k))
                v.reciprocal(rden[:, p], den[:, p]).then_inc(A[f"rden{p}"], 1)
                dve.wait_ge(A[f"rden{p}"], upto(k))
                v.tensor_tensor(attn[:, p].rearrange("q (n d) -> q n d", d=HD),
                                psO[p].rearrange("q g j d -> q (g j) d")[:, :, 0:HD],
                                rden[:, p].unsqueeze(2).broadcast_to([P, J * G, HD]),
                                ALU.mult).then_inc(A[f"o{p}"], 1)

            def output_low(k, q):
                dve.wait_ge(A["oT_hi"], upto(k))
                v.tensor_tensor(attnT_s[:, 1], psOT, attnT_s[:, 0].bitcast(F32), ALU.subtract).then_inc(A["oT_lo"], 1)

            def attention_residual(k, q):
                dve.wait_ge(A["h2b"], upto(k))
                dve.wait_ge(A["wp"], upto(k))
                v.tensor_tensor(y[:], psW, h2b[:, q], ALU.add).then_inc(A["y"], 1)

            def y_statistics(k, q):
                dve.wait_ge(A["y"], upto(k))
                statistics(y, y_stats, y_mv, A, "ystats", "ymv", k)

            def centre_y(k, q):
                dve.wait_ge(A["ymv"], upto(k))
                for p in range(2):
                    last = v.scalar_tensor_tensor(out=z[:, p], in0=y[:, p], scalar=y_mv[:, p, 0:1],
                                                  in1=gamma_rep[:], op0=ALU.subtract, op1=ALU.mult)
                last.then_inc(A["z"], 1)

            def x2_sum(k, q):
                dve.wait_ge(A["yrstd"], upto(k))
                dve.wait_ge(A["x1b"], upto(k))
                dve.wait_ge(A["z"], upto(k))
                for p in range(2):
                    last = v.scalar_tensor_tensor(out=x2[:, q, p], in0=z[:, p], scalar=y_rstd[:, p:p + 1],
                                                  in1=x1b[:, q, p], op0=ALU.mult, op1=ALU.add)
                last.then_inc(A["x2"], 1)

            def body(stage):
                stage(normalise_output, 4, 1)
                stage(normalise_output, 4, 0)
                stage(mix, 2, f1, "xr", mur)
                stage(mix, 5, f2, "xr", mur)
                stage(output_low, 4)
                stage(h2_low, 3)
                stage(x_statistics, 0)
                stage(attention_residual, 4)
                stage(y_statistics, 4)
                stage(centre_y, 4)
                stage(k_bias, 3)
                stage(v_bias, 3)
                stage(x2_sum, 4)
                stage(q_bias, 3)
                stage(x2_statistics, 4)
                stage(k_feature, 3)
                stage(gate, 5, f2)
                stage(block_diagonal_v, 3)
                stage(q_feature, 3)
                stage(low, 2, f1, "ka")
                stage(mask_state, 3)
                stage(difference, 1, f1)
                stage(mix, 1, f1, "xk", muk)
                stage(gate, 2, f1)
                stage(causal_mask, 3, 1)
                stage(mix, 4, f2, "xk", muk)
                stage(causal_mask, 3, 0)
                stage(x1_statistics, 2)
                stage(low, 4, f2, "xk")

            run(dve, body, {1: ffn_weights, 2: ffn_low_parts, 3: attention_weights, 4: output_weights})

        @block.gpsimd
        def _(pool):
            g_ = nc.gpsimd

            count = [0]

            def in_turn(ins):
                count[0] += 1
                ins.then_inc(mask_step, 1)
                pool.wait_ge(mask_step, count[0])

            def keep(t, base, pattern, channel):
                in_turn(g_.affine_select(out=t, in_=t, compare_op=ALU.is_ge, fill=0.0, base=base, pattern=pattern,
                                         channel_multiplier=channel))

            in_turn(g_.memset(ident[:], 0.0))
            g_.affine_select(out=ident[:], in_=ident[:], compare_op=ALU.not_equal, fill=1.0, base=0,
                             pattern=[[-1, P]], channel_multiplier=1).then_inc(consts, 1)
            in_turn(g_.memset(eps_ln[:], EPS_LN))
            in_turn(g_.memset(neg_one[:], -1.0))
            in_turn(g_.memset(neg_half[:], -0.5))
            for f in (f1, f2):
                in_turn(g_.memset(f.carry[:, 0], 0.0))
            g_.memset(st_carry[:, 0], 0.0).then_inc(consts, 1)
            pool.wait_ge(consts, 2)

            def ffn_weights():
                pool.wait_ge(w_hi_done, 1)
                g_.tensor_tensor(wkT[:, 1], w_full[:, 0], wkT[:, 0].bitcast(F32), ALU.subtract).then_inc(wk_lo_done, 1)

            def attention_masks():
                for t in (causal, vmask, smask, kmask):
                    in_turn(g_.memset(t[:], 1.0))
                for j in range(J):
                    keep(causal[j * C:(j + 1) * C], 0, [[1, C]], -1)
                keep(vmask[:], 0, [[-C, J], [0, HD]], 1)
                keep(vmask[:], C - 1, [[C, J], [0, HD]], -1)
                for p in range(2):
                    q = slice(p * KV, (p + 1) * KV)
                    keep(smask[q], 0, [[-HD, J], [0, V1]], 1)
                    keep(smask[q], HD - 1, [[HD, J], [0, V1]], -1)
                    keep(kmask[q], 0, [[-HD, J]], 1)
                    keep(kmask[q], HD - 1, [[HD, J]], -1)
                g_.memset(vaug[:, :, :, :, HD:], 1.0).then_inc(consts, 1)
                pool.wait_ge(consts, 3)
                pool.wait_ge(w_loaded, W_ALL)

            def inverse_deviation(s, names, mv, veps, rstd, k):
                g_.tensor_tensor(veps[:], mv[:, :, 1], eps_ln[:], ALU.add).then_inc(s[names[0]], 1)
                pool.wait_ge(s[names[0]], upto(k))
                g_.tensor_tensor(rstd[:], veps[:], neg_half[:], ALU.pow).then_inc(s[names[1]], 1)

            def norm_factors(s, mv, veps, rstd, negm, nmr, k):
                pool.wait_ge(s["mv"], upto(k))
                g_.tensor_tensor(negm[:], mv[:, :, 0], neg_one[:], ALU.mult)
                inverse_deviation(s, ("veps", "rstd"), mv, veps, rstd, k)
                pool.wait_ge(s["rstd"], upto(k))
                g_.tensor_tensor(nmr[:], negm[:], rstd[:], ALU.mult).then_inc(s["nmr"], 1)

            def x_factors(k, q):
                if has(k - 1):
                    pool.wait_ge(f1.s["h"], upto(k - 1))
                norm_factors(f1.s, f1.mv, f1.veps, f1.rstd, f1.negm, f1.nmr, k)

            def x1_factors(k, q):
                norm_factors(A, a_mv, a_veps, a_rstd, a_negm, a_nmr, k)

            def x2_factors(k, q):
                norm_factors(f2.s, f2.mv, f2.veps, f2.rstd, f2.negm, f2.nmr, k)

            def y_factors(k, q):
                pool.wait_ge(A["ymv"], upto(k))
                inverse_deviation(A, ("yveps", "yrstd"), y_mv, y_veps, y_rstd, k)

            def difference(k, q, f):
                n = k % NT
                pool.wait_ge(f.s["hT"], upto(k))
                g_.tensor_copy(f.hT[:, :, :, 0], f.carry[:, n]).then_inc(f.s["edge"], 1)
                g_.tensor_copy(f.carry[:, n + 1], f.hT[:, :, :, P])
                pool.wait_ge(f.s["edge"], upto(k))
                g_.tensor_tensor(f.d[:], f.hT[:, :, :, 1:], f.hT[:, :, :, 0:P], ALU.subtract).then_inc(f.s["d"], 1)

            def low(k, q, f, name):
                pool.wait_ge(f.s[f"{name}_hi"], upto(k))
                g_.tensor_tensor(f.split[name][:, 1], f.full[name][:], f.split[name][:, 0].bitcast(F32),
                                 ALU.subtract).then_inc(f.s[f"{name}_lo"], 1)

            def x1_sum(k, q):
                pool.wait_ge(f1.s["t1"], upto(k))
                g_.tensor_tensor(x1[:, q], x_in[:, k % NT], f1.t1[:], ALU.add).then_inc(f1.s["y"], 1)

            def x3_sum(k, q):
                if has(k - 2):
                    pool.wait_ge(stored[q], 16 * (k // 2))
                pool.wait_ge(f2.s["t1"], upto(k))
                g_.tensor_tensor(x3[:, q], x2[:, q], f2.t1[:], ALU.add).then_inc(f2.s["y"], 1)

            def h2_and_bo(k, q):
                pool.wait_ge(A["h"], upto(k))
                g_.tensor_tensor(h2b[:, q], h2[:], bo_rep[:].unsqueeze(1).broadcast_to([P, 2, D]),
                                 ALU.add).then_inc(A["h2b"], 1)

            def x1_and_beta(k, q):
                pool.wait_ge(f1.s["y"], upto(k))
                g_.tensor_tensor(x1b[:, q], x1[:, q], beta_rep[:].unsqueeze(1).broadcast_to([P, 2, D]),
                                 ALU.add).then_inc(A["x1b"], 1)

            def states(k, q):
                n = k % NT
                g_.tensor_copy(st[:, q, 0], st_carry[:, n]).then_inc(A["st0"], 1)
                pool.wait_ge(A["sp"], upto(k))
                pool.wait_ge(A["st0"], upto(k))
                g_.tensor_tensor(st[:, q, 1:], sp[:, 0:NC - 1],
                                 st[:, q, 0].unsqueeze(1).broadcast_to([P, NC - 1, VW]),
                                 ALU.add).then_inc(A["st"], 1)
                g_.tensor_tensor(st_carry[:, n + 1], sp[:, NC - 1], st[:, q, 0], ALU.add).then_inc(A["stc"], 1)

            def body(stage):
                stage(difference, 4, f2)
                stage(x1_sum, 2)
                stage(x_factors, 0)
                stage(x1_factors, 2)
                stage(low, 1, f1, "xk")
                stage(x3_sum, 5)
                stage(h2_and_bo, 2)
                stage(low, 1, f1, "xr")
                stage(low, 4, f2, "xr")
                stage(y_factors, 3)
                stage(low, 4, f2, "ka")
                stage(x1_and_beta, 2)
                stage(x2_factors, 3)
                stage(states, 2)

            run(pool, body, {1: ffn_weights, 2: attention_masks})


_INS = ['L0_attn_x', 'L0_attn_Wq', 'L0_attn_bq', 'L0_attn_Wk', 'L0_attn_bk', 'L0_attn_Wv', 'L0_attn_bv',
        'L0_attn_Wc', 'L0_attn_We', 'L0_attn_Wo', 'L0_attn_bo', 'L0_attn_gamma', 'L0_attn_beta',
        'L0_ffn_W_r', 'L0_ffn_W_k', 'L0_ffn_W_v', 'L0_ffn_mu_r', 'L0_ffn_mu_k']


def kernel(**inputs):
    import numpy as _np
    import concourse.bacc as _bacc
    from concourse import mybir as _mybir
    from concourse.bass_utils import run_bass_kernel_spmd as _run

    nc = _bacc.Bacc("TRN2", target_bir_lowering=False, num_devices=1)
    arrays, args = {}, []
    for name in _INS:
        a = _np.ascontiguousarray(inputs[name])
        arrays[f"in_{name}_dram"] = a
        args.append(nc.dram_tensor(f"in_{name}_dram", a.shape, _mybir.dt.from_np(a.dtype), kind="ExternalInput").ap())
    shape = inputs['L0_attn_x'].shape
    args.append(nc.dram_tensor("out_0_dram", shape, _mybir.dt.float32, kind="ExternalOutput").ap())
    macaron_program(nc, *args)
    r = _run(nc, [arrays], core_ids=[0])
    return r.results[0]["out_0_dram"]
```
